# Optimizing a Trainium2 kernel written in Bass

```python
import numpy as np
import jax
import jax.numpy as jnp

def _softmax(x, axis=-1):
    return jax.nn.softmax(x, axis=axis)

def _gelu(x):
    return jax.nn.gelu(x, approximate=True)

def _silu(x):
    return jax.nn.silu(x)

def _sigmoid(x):
    return jax.nn.sigmoid(x)

def _layernorm(x, axis=-1, eps=1e-05):
    m = jnp.mean(x, axis=axis, keepdims=True)
    v = jnp.var(x, axis=axis, keepdims=True)
    return (x - m) / jnp.sqrt(v + eps)

def _scatter_add(tgt, idx, src, axis=0):
    return tgt.at[idx].add(src)

def _segment_sum(src, seg, n):
    return jax.ops.segment_sum(src, seg, n)
kernel_name = 'mk_seq_preln_d1_jaxref_r4_31269d'

def setup_inputs(seed: int=0):
    np.random.seed(seed)
    _w = jnp.asarray

    def _L0_attn_setup():
        import jax, jax.numpy as jnp
        import numpy as np
        HIDDEN = 1024
        NUM_HEADS = 32
        HEAD_DIM = HIDDEN // NUM_HEADS

        def _fp8_roundtrip(x):
            return x.astype(jnp.float8_e4m3fn).astype(jnp.float32)
        key = jax.random.key(seed)
        ks = jax.random.split(key, 10)
        B, S = (2, 1024)
        hidden_states = jax.random.normal(ks[0], (B, S, HIDDEN), dtype=jnp.float32)
        scale = 0.02

        def lin(kw, kb):
            w = jax.random.normal(kw, (HIDDEN, HIDDEN), dtype=jnp.float32) * scale
            b = jax.random.normal(kb, (HIDDEN,), dtype=jnp.float32) * scale
            return (w, b)
        wq, bq = lin(ks[1], ks[2])
        wk, bk = lin(ks[3], ks[4])
        wv, bv = lin(ks[5], ks[6])
        wl, bl = lin(ks[7], ks[8])
        wq, bq = (_fp8_roundtrip(wq), _fp8_roundtrip(bq))
        wk, bk = (_fp8_roundtrip(wk), _fp8_roundtrip(bk))
        wv, bv = (_fp8_roundtrip(wv), _fp8_roundtrip(bv))
        return {'hidden_states': hidden_states, 'wq': wq, 'bq': bq, 'wk': wk, 'bk': bk, 'wv': wv, 'bv': bv, 'wl': wl, 'bl': bl}
    _L0_attn_in = _L0_attn_setup()

    def _L0_ffn_setup():
        import jax, jax.numpy as jnp
        import numpy as np
        NF4_CODE = jnp.array([-1.0, -0.6961928009986877, -0.5250730514526367, -0.39491748809814453, -0.28444138169288635, -0.18477343022823334, -0.09105003625154495, 0.0, 0.07958029955625534, 0.16093020141124725, 0.24611230194568634, 0.33791524171829224, 0.44070982933044434, 0.5626170039176941, 0.7229568362236023, 1.0], dtype=jnp.float32)
        BLOCKSIZE = 64

        def nf4_quant_dequant(w):
            shape = w.shape
            flat = w.reshape(-1, BLOCKSIZE)
            absmax = jnp.max(jnp.abs(flat), axis=1, keepdims=True)
            normalized = flat / jnp.where(absmax == 0, 1.0, absmax)
            bounds = (NF4_CODE[:-1] + NF4_CODE[1:]) * 0.5
            idx = jnp.searchsorted(bounds, normalized)
            return (NF4_CODE[idx] * absmax).reshape(shape)
        key = jax.random.key(seed)
        k1, k2, k3, kx = jax.random.split(key, 4)
        D, H = (1024, 2752)
        scale = 0.02
        w1 = jax.random.normal(k1, (H, D), jnp.float32) * scale
        w2 = jax.random.normal(k2, (H, D), jnp.float32) * scale
        w3 = jax.random.normal(k3, (D, H), jnp.float32) * scale
        x = jax.random.normal(kx, (2, 512, D), jnp.float32)
        return {'x': x, 'w1': w1, 'w2': w2, 'w3': w3}
    _L0_ffn_in = _L0_ffn_setup()
    _d = {'L0_attn_hidden_states': _L0_attn_in['hidden_states'], 'L0_attn_wq': _L0_attn_in['wq'], 'L0_attn_bq': _L0_attn_in['bq'], 'L0_attn_wk': _L0_attn_in['wk'], 'L0_attn_bk': _L0_attn_in['bk'], 'L0_attn_wv': _L0_attn_in['wv'], 'L0_attn_bv': _L0_attn_in['bv'], 'L0_attn_wl': _L0_attn_in['wl'], 'L0_attn_bl': _L0_attn_in['bl'], 'L0_ffn_w1': _L0_ffn_in['w1'], 'L0_ffn_w2': _L0_ffn_in['w2'], 'L0_ffn_w3': _L0_ffn_in['w3']}
    _x0 = _d['L0_attn_hidden_states']
    _d['L0_attn_hidden_states'] = jax.random.normal(jax.random.fold_in(jax.random.key(seed), 1), (1, 2048, 1024), dtype=_x0.dtype)
    del _x0
    return _d

def reference(L0_attn_hidden_states, L0_attn_wq, L0_attn_bq, L0_attn_wk, L0_attn_bk, L0_attn_wv, L0_attn_bv, L0_attn_wl, L0_attn_bl, L0_ffn_w1, L0_ffn_w2, L0_ffn_w3):

    def _L0_attn_ref(hidden_states, wq, bq, wk, bk, wv, bv, wl, bl):
        import jax, jax.numpy as jnp
        import numpy as np
        HIDDEN = 1024
        NUM_HEADS = 32
        HEAD_DIM = HIDDEN // NUM_HEADS

        def _fp8_roundtrip(x):
            return x.astype(jnp.float8_e4m3fn).astype(jnp.float32)
        B, S, E = hidden_states.shape
        H, D = (NUM_HEADS, HEAD_DIM)
        q = (hidden_states @ wq.T + bq).reshape(B, S, H, D)
        k = (hidden_states @ wk.T + bk).reshape(B, S, H, D)
        v = (hidden_states @ wv.T + bv).reshape(B, S, H, D)
        latent = hidden_states @ wl.T + bl
        scores = jnp.einsum('bshd,bstd->bsht', q, k) / np.sqrt(D).astype(np.float32)
        probs = jax.nn.softmax(scores, axis=-1)
        context = jnp.einsum('bsht,bstd->bshd', probs, v).reshape(B, S, E)
        return context

    def _L0_ffn_ref(x, w1, w2, w3):
        import jax, jax.numpy as jnp
        import numpy as np
        NF4_CODE = jnp.array([-1.0, -0.6961928009986877, -0.5250730514526367, -0.39491748809814453, -0.28444138169288635, -0.18477343022823334, -0.09105003625154495, 0.0, 0.07958029955625534, 0.16093020141124725, 0.24611230194568634, 0.33791524171829224, 0.44070982933044434, 0.5626170039176941, 0.7229568362236023, 1.0], dtype=jnp.float32)
        BLOCKSIZE = 64

        def nf4_quant_dequant(w):
            shape = w.shape
            flat = w.reshape(-1, BLOCKSIZE)
            absmax = jnp.max(jnp.abs(flat), axis=1, keepdims=True)
            normalized = flat / jnp.where(absmax == 0, 1.0, absmax)
            bounds = (NF4_CODE[:-1] + NF4_CODE[1:]) * 0.5
            idx = jnp.searchsorted(bounds, normalized)
            return (NF4_CODE[idx] * absmax).reshape(shape)
        dq1 = nf4_quant_dequant(w1)
        dq2 = nf4_quant_dequant(w2)
        dq3 = nf4_quant_dequant(w3)
        gate = jnp.einsum('bsd,hd->bsh', x, dq1)
        up = jnp.einsum('bsd,hd->bsh', x, dq2)
        h = jax.nn.silu(gate) * up
        return jnp.einsum('bsh,dh->bsd', h, dq3)
    x = L0_attn_hidden_states
    x = x + _L0_attn_ref(_layernorm(x, axis=-1), L0_attn_wq, L0_attn_bq, L0_attn_wk, L0_attn_bk, L0_attn_wv, L0_attn_bv, L0_attn_wl, L0_attn_bl)
    x = x + _L0_ffn_ref(_layernorm(x, axis=-1), L0_ffn_w1, L0_ffn_w2, L0_ffn_w3)
    return x

_drawn_inputs = setup_inputs


def setup_inputs(seed=0):
    import zlib

    import numpy as np

    out = dict(_drawn_inputs(seed))
    spreads = {}
    factors = {'L0_attn_bq': 32.693, 'L0_attn_bk': 22.291, 'L0_attn_bv': 8.0}
    for name, (base, spread) in spreads.items():
        noise = np.random.default_rng([zlib.crc32(name.encode()), seed]).standard_normal(out[name].shape)
        drawn = base * np.exp(spread * noise) if base else spread * noise
        out[name] = jnp.asarray(drawn.astype(out[name].dtype))
    for name, factor in factors.items():
        out[name] = (out[name] * factor).astype(out[name].dtype)
    return out
```

```python
from contextlib import ExitStack

import numpy as np

import concourse.bass as bass
from concourse import mybir

F32 = mybir.dt.float32
F16 = mybir.dt.float16
I32 = mybir.dt.int32
I8 = mybir.dt.int8
ALU = mybir.AluOpType
ACT = mybir.ActivationFunctionType
AX = mybir.AxisListType
ALL_MAX = bass.bass_isa.ReduceOp.max

P = 128
QUAD = 32
BANK = 512
EPS = 1e-5
X_SCALE = 2.0 ** 10
TINY = 2.0 ** -60
EXPONENT_BITS = 0x7F800000
BLOCK = 64

NF4 = np.array([-1.0, -0.6961928009986877, -0.5250730514526367, -0.39491748809814453,
                -0.28444138169288635, -0.18477343022823334, -0.09105003625154495, 0.0,
                0.07958029955625534, 0.16093020141124725, 0.24611230194568634,
                0.33791524171829224, 0.44070982933044434, 0.5626170039176941,
                0.7229568362236023, 1.0], dtype=np.float32)
LEVELS = len(NF4) - 1
BOUNDS = (NF4[:-1] + NF4[1:]) * np.float32(0.5)


def strict_compare(bound):
    b = np.float64(bound)
    middle = (b + np.float64(np.nextafter(bound, np.float32(2.0)))) / 2
    best = None
    for k in range(2000):
        scale = np.float32(1.0 + k * 2.0 ** -23)
        bias = np.float32(np.float64(scale) * middle)
        off = abs(np.float64(bias) / np.float64(scale) - middle)
        if best is None or off < best[0]:
            best = (off, float(scale), -float(bias))
    return best[1], best[2]


COMPARE = [strict_compare(b) for b in BOUNDS]
GRID = 2.0 ** 25
HALF_STEP = [float(np.round((np.float64(NF4[i + 1]) - np.float64(NF4[i])) / 2 * GRID) / GRID)
             for i in range(LEVELS)]
SIGN_RING = 5



class Count:

    def __init__(self, sem):
        self.sem, self.base, self.off = sem, 0, 0

    def at(self, base):
        self.base, self.off = base, 0

    def mark(self, ins):
        self.off += 1
        return ins.then_inc(self.sem, 1)

    def wait(self, eng):
        eng.wait_ge(self.sem, self.base + self.off)


def layer(nc, x, wq, bq, wk, bk, wv, bv, w1, w2, w3, out):
    TOK, E = x.shape[-2:]
    FF = w1.shape[0]
    HD = QUAD
    HEADS = E // HD
    C = E // P
    T = TOK // P
    SB = TOK // BANK
    FT = FF // P
    REST = FF - FT * P
    NB = E // BLOCK
    HALVES = E // BANK
    GROUP = 2
    UNITS = 3 * (FT + 1)
    x_dram = x.rearrange("a s e -> (a s) e")
    x1_dram = nc.dram_tensor("x1", [TOK, E], F32).ap()

    with ExitStack() as whole:
        def sem(name):
            return whole.enter_context(nc.semaphore(name))

        def keep(name, shape, dt=F32):
            return whole.enter_context(nc.sbuf_tensor(name, shape, dt))

        bank = whole.enter_context(nc.psum_tensor("bank", [P, 8, BANK], F32))

        ident = keep("ident", [P, P])
        compare_bias = keep("compare_bias", [P, LEVELS])
        power = keep("power", [P, 2])
        absmax = keep("absmax", [P, FT + 1, 3, NB])
        inv_absmax = keep("inv_absmax", [P, FT + 1, 3, NB])
        top = keep("top", [P, 4])
        top_all = keep("top_all", [P, 4])
        pow2 = keep("pow2", [P, 4])
        inv_pow2 = keep("inv_pow2", [P, 4])
        w_scale = keep("w_scale", [P, 4])
        un_scale = keep("un_scale", [P, 4])
        stats = keep("stats", [P, 2, 6])
        mean_var = keep("mean_var", [P, 2])
        var_eps = keep("var_eps", [P, 1])
        rstd = keep("rstd", [P, 1])
        row_max = keep("row_max", [P, QUAD])
        row_sum = keep("row_sum", [P, QUAD])
        inv_sum = keep("inv_sum", [P, QUAD])

        consts_set = sem("consts_set")
        dve_seq = sem("dve_seq")

        attention(nc, locals())
        acc = keep("acc", [P, T, E])
        x2T_hi = keep("x2T_hi", [P, C, TOK], F16)
        x2T_lo = keep("x2T_lo", [P, C, TOK], F16)
        second_norm(nc, locals())
        feed_forward(nc, locals())


def attention(nc, g):
    C, T, E, NB, FT, REST, HEADS, HD, HALVES = (g[k] for k in "C T E NB FT REST HEADS HD HALVES".split())
    bank, ident, sem = g["bank"], g["ident"], g["sem"]
    top, top_all, pow2, inv_pow2, w_scale, un_scale = (g[k] for k in "top top_all pow2 inv_pow2 w_scale un_scale".split())
    stats, mean_var, var_eps, rstd = (g[k] for k in "stats mean_var var_eps rstd".split())
    row_max, row_sum, inv_sum, absmax = (g[k] for k in "row_max row_sum inv_sum absmax".split())
    power, compare_bias, consts_set, dve_seq = (g[k] for k in "power compare_bias consts_set dve_seq".split())
    x_dram, x1_dram = g["x_dram"], g["x1_dram"]
    w_qkv = [g["wq"], g["wk"], g["wv"]]
    b_qkv = [g["bq"], g["bk"], g["bv"]]
    w1, w2, w3 = g["w1"], g["w2"], g["w3"]
    seq = Count(dve_seq)

    with ExitStack() as mine:
        def sb(name, shape, dt=F32):
            return mine.enter_context(nc.sbuf_tensor(name, shape, dt))

        wT_hi = sb("wT_hi", [P, C, 3, E], F16)
        wT_lo = sb("wT_lo", [P, C, 3, E], F16)

        w_in = [sem(f"w_in{m}") for m in range(3)]
        local_max = sem("local_max")
        global_max = sem("global_max")
        scale_set = sem("scale_set")
        w_turned = sem("w_turned")
        w_hi_done = sem("w_hi_done")
        w_lo_done = sem("w_lo_done")

        RING = 4
        FILLS = C * 2
        with nc.sbuf_tensor("w_raw", [P, 3, C, E], F32) as w_raw, nc.Block() as block:

            @block.sync
            def _(sp):
                for m in range(3):
                    sp.dma_start(w_raw[:, m], w_qkv[m].rearrange("(t p) d -> p t d", p=P)).then_inc(w_in[m], 16)

            @block.gpsimd
            def _(pool):
                pool.memset(ident[:], 0.0).then_inc(consts_set, 1)
                pool.memset(absmax[:], 0.0).then_inc(consts_set, 1)
                pool.memset(power[:, 0:1], -0.5).then_inc(consts_set, 1)
                pool.memset(power[:, 1:2], 0.5).then_inc(consts_set, 1)
                for i in range(LEVELS):
                    pool.memset(compare_bias[:, i:i + 1], COMPARE[i][1]).then_inc(consts_set, 1)
                pool.wait_ge(consts_set, 1)
                pool.affine_select(out=ident[:], in_=ident[:], compare_op=ALU.not_equal, fill=1.0, base=0,
                                   pattern=[[-1, P]], channel_multiplier=1).then_inc(consts_set, 1)
                for m in range(3):
                    pool.wait_ge(local_max, m + 1)
                    nc.gpsimd.partition_all_reduce(top_all[:, m:m + 1], top[:, m:m + 1], P, ALL_MAX).then_inc(global_max, 1)

            @block.vector
            def _(dve):
                for m in range(3):
                    col = slice(m, m + 1)
                    dve.wait_ge(w_in[m], 16)
                    nc.vector.tensor_reduce(top[:, col], w_raw[:, m].rearrange("p t d -> p (t d)"), AX.X, ALU.max,
                                            apply_absolute_value=True).then_inc(local_max, 1)
                    dve.wait_ge(global_max, m + 1)
                    seq.mark(nc.vector.tensor_scalar(pow2[:, col], top_all[:, col], TINY, None, ALU.max))
                    seq.wait(dve)
                    seq.mark(nc.vector.tensor_scalar(pow2[:, col].bitcast(I32), pow2[:, col].bitcast(I32),
                                                     EXPONENT_BITS, None, ALU.bitwise_and))
                    seq.wait(dve)
                    seq.mark(nc.vector.reciprocal(inv_pow2[:, col], pow2[:, col]))
                    seq.mark(nc.vector.tensor_scalar(un_scale[:, col], pow2[:, col], 2.0 ** -14 / X_SCALE, None, ALU.mult))
                    seq.wait(dve)
                    nc.vector.tensor_scalar(w_scale[:, col], inv_pow2[:, col], 2.0 ** 14, None, ALU.mult).then_inc(scale_set, 1)
                    dve.wait_ge(scale_set, m + 1)
                    for f in range(FILLS):
                        n = m * FILLS + f
                        c, half = f // 2, f % 2
                        dst = (slice(None), c, m, slice(half * BANK, half * BANK + BANK))
                        dve.wait_ge(w_hi_done, n + 1)
                        nc.vector.scalar_tensor_tensor(wT_lo[dst], bank[:, n % RING], w_scale[:, col], wT_hi[dst],
                                                       ALU.mult, ALU.subtract).then_inc(w_lo_done, 1)

            @block.scalar
            def _(act):
                for m in range(3):
                    act.wait_ge(scale_set, m + 1)
                    for f in range(FILLS):
                        n = m * FILLS + f
                        c, half = f // 2, f % 2
                        act.wait_ge(w_turned, n + 1)
                        nc.scalar.activation(wT_hi[:, c, m, half * BANK:half * BANK + BANK], bank[:, n % RING],
                                             ACT.Copy, scale=w_scale[:, m:m + 1]).then_inc(w_hi_done, 1)

            @block.tensor
            def _(pe):
                pe.wait_ge(consts_set, 5 + LEVELS)
                for m in range(3):
                    pe.wait_ge(w_in[m], 16)
                    for f in range(FILLS):
                        n = m * FILLS + f
                        c, half = f // 2, f % 2
                        if n >= RING:
                            pe.wait_ge(w_lo_done, n - RING + 1)
                        for j in range(BANK // P):
                            t = half * (BANK // P) + j
                            last = nc.tensor.transpose(bank[:, n % RING, j * P:(j + 1) * P],
                                                       w_raw[:, m, t, c * P:(c + 1) * P], ident[:])
                        last.then_inc(w_turned, 1)

        bias = sb("bias", [P, 3, E])
        x_nat = sb("x_nat", [P, 2, E])
        x_res = sb("x_res", [P, E])
        xT_hi = sb("xT_hi", [P, 2, C, P], F16)
        xT_lo = sb("xT_lo", [P, 2, C, P], F16)
        qkv = sb("qkv", [P, 3, E])
        q_diag = sb("q_diag", [P, QUAD, P])
        p_diag = sb("p_diag", [P, QUAD, P])
        kT = sb("kT", [P, QUAD, HEADS])
        vT = sb("vT", [P, QUAD, HD])
        probs = sb("probs", [P, QUAD, HEADS])
        ctx_nat = sb("ctx_nat", [P, E])
        ff_raw = sb("ff_raw", [P, E])

        bias_in = sem("bias_in")
        diag_zero = sem("diag_zero")
        x_in = [sem("x_in0"), sem("x_in1")]
        res_in = sem("res_in")
        var_ready = sem("var_ready")
        rstd_ready = sem("rstd_ready")
        normed = sem("normed")
        x_turned = sem("x_turned")
        x_hi_done = sem("x_hi_done")
        x_lo_done = sem("x_lo_done")
        projected = [sem("projected0"), sem("projected1")]
        evacuated = [sem("evacuated0"), sem("evacuated1")]
        qk_ready = sem("qk_ready")
        v_ready = sem("v_ready")
        scores_done = sem("scores_done")
        centered = sem("centered")
        exp_done = sem("exp_done")
        p_ready = sem("p_ready")
        context_done = sem("context_done")
        ctx_ready = sem("ctx_ready")
        res_done = sem("res_done")
        x1_out = sem("x1_out")
        ff_in = sem("ff_in")
        held = sem("held")
        absmax_done = sem("absmax_done")

        scores = bank[:, 2:4].rearrange("p b n -> p (b n)").rearrange("p (t h) -> p t h", h=HEADS)
        context = bank[:, 4:6].rearrange("p b n -> p (b n)").rearrange("p (t d) -> p t d", d=HD)
        MARKS = 6
        FF_STEP = (5, 4)

        with nc.Block() as block:

            @block.sync
            def _(sp):
                def load_x(n, slot):
                    sp.dma_start(x_nat[:, slot], x_dram[bass.ds(n * P, P), :]).then_inc(x_in[slot], 16)

                def store_x1(n):
                    sp.wait_ge(res_done, n + 1)
                    sp.dma_start(x1_dram[bass.ds(n * P, P), :], x_res[:]).then_inc(x1_out, 16)

                def load_res(n):
                    sp.wait_ge(x1_out, n * 16)
                    sp.dma_start(x_res[:], x_dram[bass.ds(n * P, P), :]).then_inc(res_in, 16)

                def load_ff(tile, m, j, rows):
                    first = tile * P
                    sp.wait_ge(absmax_done, j)
                    if m == 2:
                        sp.sem_inc(held, 1)
                    if m < 2:
                        sp.dma_start(ff_raw[0:rows], (w1, w2)[m][bass.ds(first, rows), :]).then_inc(ff_in, 16)
                    else:
                        sp.dma_start(ff_raw[:, 0:C * rows].rearrange("p (t h) -> p t h", t=C),
                                     w3.rearrange("(t p) h -> p t h", p=P)[:, :, bass.ds(first, rows)]).then_inc(ff_in, 16)

                for m in range(3):
                    sp.dma_start(bias[:, m], b_qkv[m].rearrange("(o n) -> o n", o=1).to_broadcast([P, E])).then_inc(bias_in, 16)
                load_x(0, 0)
                load_x(1, 1)
                load_res(0)
                with sp.Fori(0, (T - 2) // 2) as it:
                    for u in range(2):
                        n = it * 2 + 1 + u
                        if u == 1:
                            store_x1(n - 2)
                            load_res(n - 1)
                        else:
                            pass
                        sp.wait_ge(x_turned, 2 * n)
                        load_x(n + 1, (u + 2) % 2)
                        for k in range(FF_STEP[u]):
                            pos = u * FF_STEP[0] + k
                            load_ff(it * 3 + pos // 3, pos % 3, it * 9 + pos, P)
                        if u == 1:
                            store_x1(n - 1)
                            load_res(n)
                for m in range(3):
                    load_ff(FT, m, 3 * FT + m, REST)
                store_x1(T - 2)
                load_res(T - 1)
                store_x1(T - 1)
                sp.wait_ge(x1_out, 16 * T)

            @block.gpsimd
            def _(pool):
                pool.memset(q_diag[:], 0.0).then_inc(diag_zero, 1)
                pool.memset(p_diag[:], 0.0).then_inc(diag_zero, 1)

                def inv_std(n):
                    pool.wait_ge(var_ready, n + 1)
                    nc.gpsimd.tensor_tensor(rstd[:], var_eps[:], power[:, 0:1], ALU.pow).then_inc(rstd_ready, 1)

                def residual(n):
                    pool.wait_ge(ctx_ready, n + 1)
                    pool.wait_ge(res_in, 16 * (n + 1))
                    nc.gpsimd.tensor_tensor(x_res[:], x_res[:], ctx_nat[:], ALU.add).then_inc(res_done, 1)

                inv_std(0)
                inv_std(1)
                with pool.Fori(0, (T - 2) // 2) as it:
                    for u in range(2):
                        n = it * 2 + 1 + u
                        inv_std(n + 1)
                        residual(n - 1)
                residual(T - 2)
                residual(T - 1)

            @block.vector
            def _(dve):
                def norm(n, slot, use):
                    dve.wait_ge(x_in[slot], 16 * (use + 1))
                    for h in range(2):
                        last = nc.vector.bn_stats(stats[:, h], x_nat[:, slot, h * BANK:(h + 1) * BANK])
                    seq.mark(last)
                    seq.wait(dve)
                    dve.sem_inc(held, 1)
                    seq.mark(nc.vector.bn_aggr(mean_var[:], stats[:].rearrange("p h s -> p (h s)")))
                    seq.wait(dve)
                    nc.vector.tensor_scalar(var_eps[:], mean_var[:, 1:2], EPS, None, ALU.add).then_inc(var_ready, 1)
                    dve.wait_ge(rstd_ready, n + 1)
                    nc.vector.tensor_scalar(x_nat[:, slot], x_nat[:, slot], mean_var[:, 0:1], rstd[:, 0:1],
                                            ALU.subtract, ALU.mult).then_inc(normed, 1)

                def split_lo(n, slot):
                    for h in range(2):
                        dve.wait_ge(x_hi_done, 2 * n + h + 1)
                        rows = xT_hi[:, slot, 4 * h:4 * h + 4].rearrange("p c s -> p (c s)")
                        nc.vector.scalar_tensor_tensor(xT_lo[:, slot, 4 * h:4 * h + 4].rearrange("p c s -> p (c s)"),
                                                       bank[:, 6 + h], X_SCALE, rows, ALU.mult, ALU.subtract).then_inc(x_lo_done, 1)

                def evacuate(n, m, h):
                    cols = slice(h * BANK, (h + 1) * BANK)
                    dve.wait_ge(projected[h], 3 * n + m + 1)
                    nc.vector.scalar_tensor_tensor(qkv[:, m, cols], bank[:, h], un_scale[:, m:m + 1], bias[:, m, cols],
                                                   ALU.mult, ALU.add).then_inc(evacuated[h], 1)

                def all_of(n, m):
                    for h in range(2):
                        dve.wait_ge(evacuated[h], 3 * n + m + 1)

                def turn_q_k(n):
                    all_of(n, 0)
                    for a in range(P // QUAD):
                        rows = slice(a * QUAD, (a + 1) * QUAD)
                        nc.vector.transpose(q_diag[rows, :, rows].rearrange("p t h -> p h t"),
                                            qkv[rows, 0].rearrange("p (h d) -> p h d", d=HD))
                    all_of(n, 1)
                    nc.vector.transpose(kT[:].rearrange("p t h -> p h t"),
                                        qkv[:, 1].rearrange("p (h d) -> p h d", d=HD)).then_inc(qk_ready, 1)

                def turn_v(n):
                    all_of(n, 2)
                    nc.vector.transpose(vT[:].rearrange("p t d -> p d t"),
                                        qkv[:, 2].rearrange("p (h d) -> p d h", d=HD)).then_inc(v_ready, 1)

                def center(n):
                    dve.wait_ge(scores_done, n + 1)
                    seq.mark(nc.vector.tensor_reduce(row_max[:], scores, AX.X, ALU.max))
                    seq.wait(dve)
                    nc.vector.tensor_tensor(probs[:], scores, row_max[:].unsqueeze(2).to_broadcast([P, QUAD, HEADS]),
                                            ALU.subtract).then_inc(centered, 1)

                def turn_p(n):
                    dve.wait_ge(exp_done, n + 1)
                    seq.mark(nc.vector.tensor_reduce(row_sum[:], probs[:], AX.X, ALU.add))
                    seq.wait(dve)
                    seq.mark(nc.vector.reciprocal(inv_sum[:], row_sum[:]))
                    for a in range(P // QUAD):
                        rows = slice(a * QUAD, (a + 1) * QUAD)
                        last = nc.vector.transpose(p_diag[rows, :, rows], probs[rows])
                    last.then_inc(p_ready, 1)

                def finish(n):
                    dve.wait_ge(context_done, n + 1)
                    seq.wait(dve)
                    seq.mark(nc.vector.tensor_tensor(probs[:], context, inv_sum[:].unsqueeze(2).to_broadcast([P, QUAD, HD]),
                                                     ALU.mult))
                    seq.wait(dve)
                    dve.wait_ge(res_done, n)
                    nc.vector.transpose(ctx_nat[:].rearrange("p (h d) -> p d h", d=HD),
                                        probs[:].rearrange("p t d -> p d t")).then_inc(ctx_ready, 1)

                def look(out_cols, j, rows, blocks):
                    dve.wait_ge(ff_in, 16 * (j + 1))
                    nc.vector.tensor_reduce(out_cols, ff_raw[0:rows, 0:blocks * BLOCK].rearrange("p (b e) -> p b e", e=BLOCK),
                                            AX.X, ALU.max, apply_absolute_value=True).then_inc(absmax_done, 1)

                flat = absmax[:].rearrange("p t m b -> p (t m b)")

                def step(n, slot, use, project=True, attend=True, normalize=True, ff=()):
                    ff = list(ff)

                    def look_at_next():
                        if ff:
                            look(*ff.pop(0))
                    if project:
                        evacuate(n, 0, 0)
                        evacuate(n, 0, 1)
                    if attend:
                        center(n - 1)
                    look_at_next()
                    if normalize:
                        norm(n + 1, 1 - slot, use)
                    if project:
                        evacuate(n, 1, 0)
                    if attend:
                        turn_p(n - 1)
                    if project:
                        evacuate(n, 1, 1)
                    look_at_next()
                    if normalize:
                        split_lo(n + 1, 1 - slot)
                    if project:
                        turn_q_k(n)
                        evacuate(n, 2, 0)
                        look_at_next()
                        evacuate(n, 2, 1)
                    look_at_next()
                    if attend:
                        finish(n - 1)
                    look_at_next()
                    if project:
                        turn_v(n)

                dve.wait_ge(consts_set, 5 + LEVELS)
                seq.at(3 * 4)
                norm(0, 0, 0)
                split_lo(0, 0)
                dve.wait_ge(diag_zero, 2)
                dve.wait_ge(bias_in, 48)
                step(0, 0, 0, attend=False)
                before = 3 * 4 + 2 + 2
                with dve.Fori(0, (T - 2) // 2) as it:
                    for u in range(2):
                        n = it * 2 + 1 + u
                        seq.at(before + it * (2 * MARKS) + u * MARKS)
                        todo = [(flat[:, bass.ds((it * 9 + u * FF_STEP[0] + k) * NB, NB)], it * 9 + u * FF_STEP[0] + k, P, NB)
                                for k in range(FF_STEP[u])]
                        step(n, 1 - u, it + 1, ff=todo)
                        assert seq.off == MARKS
                seq.at(before + (T - 2) * MARKS)
                todo = [(absmax[0:REST, FT, 0], 3 * FT, REST, NB), (absmax[0:REST, FT, 1], 3 * FT + 1, REST, NB),
                        (absmax[:, FT, 2, 0::P // REST], 3 * FT + 2, P, NB * REST // P)]
                step(T - 1, 1, 0, normalize=False, ff=todo)
                step(T, 0, 0, project=False, normalize=False)
                dve.wait_ge(absmax_done, 3 * FT + 3)

            @block.scalar
            def _(act):
                def split_hi(n, slot):
                    for h in range(2):
                        act.wait_ge(x_turned, 2 * n + h + 1)
                        nc.scalar.activation(xT_hi[:, slot, 4 * h:4 * h + 4].rearrange("p c s -> p (c s)"), bank[:, 6 + h],
                                             ACT.Copy, scale=X_SCALE).then_inc(x_hi_done, 1)

                def exponentials(n):
                    act.wait_ge(centered, n + 1)
                    flat = probs[:].rearrange("p t h -> p (t h)")
                    nc.scalar.activation(flat, flat, ACT.Exp, scale=float(1 / np.sqrt(np.float32(HD)))).then_inc(exp_done, 1)

                split_hi(0, 0)
                split_hi(1, 1)
                with act.Fori(0, (T - 2) // 2) as it:
                    for u in range(2):
                        n = it * 2 + 1 + u
                        exponentials(n - 1)
                        split_hi(n + 1, u)
                exponentials(T - 2)
                exponentials(T - 1)

            @block.tensor
            def _(pe):
                def turn_x(n, slot):
                    pe.wait_ge(normed, n + 1)
                    for h in range(2):
                        pe.wait_ge(x_lo_done, 2 * n)
                        for c in range(4 * h, 4 * h + 4):
                            last = nc.tensor.transpose(bank[:, 6 + h, (c % 4) * P:(c % 4 + 1) * P],
                                                       x_nat[:, slot, c * P:(c + 1) * P], ident[:])
                        last.then_inc(x_turned, 1)

                def project(n, slot, m):
                    pe.wait_ge(x_lo_done, 2 * n + 2)
                    for h in range(2):
                        cols = slice(h * BANK, (h + 1) * BANK)
                        pe.wait_ge(evacuated[h], 3 * n + m)
                        for c in range(C):
                            nc.tensor.matmul(bank[:, h], xT_hi[:, slot, c], wT_hi[:, c, m, cols], start=c == 0, stop=False)
                            nc.tensor.matmul(bank[:, h], xT_hi[:, slot, c], wT_lo[:, c, m, cols], start=False, stop=False)
                            last = nc.tensor.matmul(bank[:, h], xT_lo[:, slot, c], wT_hi[:, c, m, cols], start=False, stop=c == C - 1)
                        last.then_inc(projected[h], 1)

                def score(n):
                    pe.wait_ge(qk_ready, n + 1)
                    for t in range(QUAD):
                        last = nc.tensor.matmul(scores[:, t], q_diag[:, t], kT[:, t], start=True, stop=True)
                    last.then_inc(scores_done, 1)

                def mix(n):
                    pe.wait_ge(p_ready, n + 1)
                    pe.wait_ge(v_ready, n + 1)
                    for t in range(QUAD):
                        last = nc.tensor.matmul(context[:, t], p_diag[:, t], vT[:, t], start=True, stop=True)
                    last.then_inc(context_done, 1)

                def step(n, slot, attend=True, normalize=True):
                    project(n, slot, 0)
                    if attend:
                        score(n - 1)
                    project(n, slot, 1)
                    if normalize:
                        turn_x(n + 1, 1 - slot)
                    project(n, slot, 2)
                    if attend:
                        mix(n - 1)

                turn_x(0, 0)
                step(0, 0, attend=False)
                with pe.Fori(0, (T - 2) // 2) as it:
                    for u in range(2):
                        step(it * 2 + 1 + u, 1 - u)
                step(T - 1, 1, normalize=False)
                score(T - 1)
                mix(T - 1)



def second_norm(nc, g):
    C, T, E, NB, FT = (g[k] for k in "C T E NB FT".split())
    bank, ident, sem = g["bank"], g["ident"], g["sem"]
    absmax, inv_absmax = g["absmax"], g["inv_absmax"]
    top, top_all, pow2, inv_pow2, w_scale, un_scale = (g[k] for k in "top top_all pow2 inv_pow2 w_scale un_scale".split())
    stats, mean_var, var_eps, rstd, power = (g[k] for k in "stats mean_var var_eps rstd power".split())
    acc, x2T_hi, x2T_lo, x1_dram = (g[k] for k in "acc x2T_hi x2T_lo x1_dram".split())

    with ExitStack() as mine:
        squares = mine.enter_context(nc.sbuf_tensor("squares", [P, FT + 1, 2, NB], F32))
        norms = mine.enter_context(nc.sbuf_tensor("norms", [P, FT + 1, 2], F32))
        norm_prod = mine.enter_context(nc.sbuf_tensor("norm_prod", [P, FT + 1], F32))
        x_norm = mine.enter_context(nc.sbuf_tensor("x_norm", [P, 2, E], F32))
        seq = Count(sem("dve_seq2"))
        ff_max = sem("ff_max")
        ff_max_all = sem("ff_max_all")
        ff_root = sem("ff_root")
        ff_floor = sem("ff_floor")
        held = sem("held2")
        x1_in = [sem("x1_in0"), sem("x1_in1")]
        var_ready = sem("var_ready2")
        rstd_ready = sem("rstd_ready2")
        normed = sem("normed2")
        turned = sem("turned2")
        hi_done = sem("hi_done2")
        lo_done = sem("lo_done2")
        SCALE_MARKS = 18
        block = mine.enter_context(nc.Block())

        @block.sync
        def _(sp):
            with sp.Fori(0, T // 2) as it:
                for u in range(2):
                    n = it * 2 + u
                    sp.wait_ge(turned, it * 4)
                    sp.dma_start(acc[:, bass.ds(n, 1)].rearrange("p o e -> p (o e)"), x1_dram[bass.ds(n * P, P), :]).then_inc(x1_in[u], 16)

        @block.gpsimd
        def _(pool):
            pool.wait_ge(ff_max, 1)
            nc.gpsimd.partition_all_reduce(top_all[:], top[:], P, ALL_MAX).then_inc(ff_max_all, 1)
            pool.wait_ge(ff_floor, 1)
            nc.gpsimd.tensor_tensor(top_all[:, 3:4], pow2[:, 3:4], power[:, 1:2], ALU.pow).then_inc(ff_root, 1)
            with pool.Fori(0, T // 2) as it:
                for u in range(2):
                    pool.wait_ge(var_ready, it * 2 + u + 1)
                    nc.gpsimd.tensor_tensor(rstd[:], var_eps[:], power[:, 0:1], ALU.pow).then_inc(rstd_ready, 1)

        @block.vector
        def _(dve):
            V = nc.vector

            def then(ins):
                seq.mark(ins)
                seq.wait(dve)

            for m in range(3):
                then(V.tensor_reduce(top[:, m:m + 1], absmax[:, :, m], AX.XY, ALU.max))
            then(V.tensor_tensor(squares[:], absmax[:, :, 0:2], absmax[:, :, 0:2], ALU.mult))
            then(V.tensor_reduce(norms[:], squares[:], AX.X, ALU.add))
            then(V.tensor_tensor(norm_prod[:], norms[:, :, 0], norms[:, :, 1], ALU.mult))
            V.tensor_reduce(top[:, 3:4], norm_prod[:], AX.X, ALU.max).then_inc(ff_max, 1)
            then(V.tensor_scalar(inv_absmax[:], absmax[:], TINY, None, ALU.max))
            then(V.reciprocal(inv_absmax[:], inv_absmax[:]))
            dve.wait_ge(ff_max_all, 1)
            V.tensor_scalar(pow2[:], top_all[:], TINY, None, ALU.max).then_inc(ff_floor, 1)
            dve.wait_ge(ff_root, 1)
            then(V.tensor_copy(pow2[:, 3:4], top_all[:, 3:4]))
            then(V.tensor_scalar(pow2[:].bitcast(I32), pow2[:].bitcast(I32), EXPONENT_BITS, None, ALU.bitwise_and))
            then(V.reciprocal(inv_pow2[:], pow2[:]))
            then(V.tensor_scalar(w_scale[:, 0:3], inv_pow2[:, 0:3], 2.0 ** 14, None, ALU.mult))
            for m in range(3):
                then(V.tensor_scalar(absmax[:, :, m], absmax[:, :, m], w_scale[:, m:m + 1], None, ALU.mult))
            then(V.tensor_scalar(un_scale[:, 0:2], pow2[:, 0:2], 2.0 ** -14 / X_SCALE, None, ALU.mult))
            then(V.tensor_scalar(un_scale[:, 1:2], un_scale[:, 1:2], inv_pow2[:, 3:4], 2.0 ** -2, ALU.mult, ALU.mult))
            then(V.tensor_scalar(un_scale[:, 2:3], pow2[:, 2:3], pow2[:, 3:4], 2.0 ** (2 - 14), ALU.mult, ALU.mult))
            assert seq.off == SCALE_MARKS, seq.off

            with dve.Fori(0, T // 2) as it:
                for u in range(2):
                    n = it * 2 + u
                    seq.at(SCALE_MARKS + it * 4 + u * 2)
                    row = acc[:, bass.ds(n, 1)].rearrange("p o e -> p (o e)")
                    dve.wait_ge(x1_in[u], 16 * (it + 1))
                    for h in range(2):
                        last = V.bn_stats(stats[:, h], acc[:, bass.ds(n, 1), h * BANK:(h + 1) * BANK].rearrange("p o e -> p (o e)"))
                    then(last)
                    dve.sem_inc(held, 1)
                    then(V.bn_aggr(mean_var[:], stats[:].rearrange("p h s -> p (h s)")))
                    V.tensor_scalar(var_eps[:], mean_var[:, 1:2], EPS, None, ALU.add).then_inc(var_ready, 1)
                    dve.wait_ge(rstd_ready, n + 1)
                    dve.wait_ge(turned, it * 4)
                    V.tensor_scalar(x_norm[:, u], row, mean_var[:, 0:1], rstd[:, 0:1], ALU.subtract, ALU.mult).then_inc(normed, 1)
                    for h in range(2):
                        dve.wait_ge(hi_done, 2 * n + h + 1)
                        dst = (slice(None), slice(4 * h, 4 * h + 4), bass.ds(n * P, P))
                        V.scalar_tensor_tensor(x2T_lo[dst], bank[:, 2 * u + h].rearrange("p (c s) -> p c s", s=P), X_SCALE,
                                               x2T_hi[dst], ALU.mult, ALU.subtract).then_inc(lo_done, 1)

        @block.scalar
        def _(act):
            with act.Fori(0, T // 2) as it:
                for u in range(2):
                    n = it * 2 + u
                    for h in range(2):
                        act.wait_ge(turned, 2 * n + h + 1)
                        nc.scalar.activation(x2T_hi[:, 4 * h:4 * h + 4, bass.ds(n * P, P)],
                                             bank[:, 2 * u + h].rearrange("p (c s) -> p c s", s=P), ACT.Copy,
                                             scale=X_SCALE).then_inc(hi_done, 1)

        @block.tensor
        def _(pe):
            with pe.Fori(0, T // 2) as it:
                for u in range(2):
                    n = it * 2 + u
                    pe.wait_ge(normed, n + 1)
                    pe.wait_ge(lo_done, it * 4)
                    for h in range(2):
                        for c in range(4):
                            last = nc.tensor.transpose(bank[:, 2 * u + h, c * P:(c + 1) * P],
                                                       x_norm[:, u, (4 * h + c) * P:(4 * h + c + 1) * P], ident[:])
                        last.then_inc(turned, 1)


def feed_forward(nc, g):
    C, T, E, NB, FT, REST, SB, HALVES, GROUP, UNITS = (g[k] for k in "C T E NB FT REST SB HALVES GROUP UNITS".split())
    bank, ident, sem = g["bank"], g["ident"], g["sem"]
    absmax, inv_absmax, un_scale, compare_bias = (g[k] for k in "absmax inv_absmax un_scale compare_bias".split())
    acc, x2T_hi, x2T_lo, out = (g[k] for k in "acc x2T_hi x2T_lo out".split())
    w1, w2, w3 = g["w1"], g["w2"], g["w3"]
    out_dram = out.rearrange("a s e -> (a s) e")
    GATE, UP, TURN, DOWN = 0, 2, 4, 6
    ROUNDS = (FT + 1) // GROUP
    ST_BLOCK = BANK // P

    UNIT = ((0, 0), (1, 0), (0, 1), (1, 1), (2, 0), (2, 1), (0, 2), (1, 2), (0, 3))
    AHEAD = 3
    WINDOWS = 6

    with ExitStack() as mine:
        def sb(name, shape, dt=F32):
            return mine.enter_context(nc.sbuf_tensor(name, shape, dt))

        w12T_hi = sb("w12T_hi", [P, 2, 2, C, P], F16)
        w12T_lo = sb("w12T_lo", [P, 2, 2, C, P], F16)
        w3T_hi = sb("w3T_hi", [P, 2, E], F16)
        w3T_lo = sb("w3T_lo", [P, 2, E], F16)
        hT_hi = sb("hT_hi", [P, 2, SB * BANK], F16)
        hT_lo = sb("hT_lo", [P, 2, SB * BANK], F16)
        w_nat = sb("w_nat", [P, 2, E])
        codes = sb("codes", [P, 2, E])
        signs = sb("signs", [P, SIGN_RING, E], I8)
        hidden = sb("hidden", [P, 2, BANK])

        w_in = [sem("ffw_in0"), sem("ffw_in1")]
        divided = sem("divided")
        held = sem("held3")
        sign_set = sem("sign_set")
        sign_used = sem("sign_used")
        rounded = sem("rounded")
        w_turned = sem("ffw_turned")
        w_hi_done = sem("ffw_hi_done")
        w_lo_done = sem("ffw_lo_done")
        gate_done = sem("gate_done")
        up_done = sem("up_done")
        silu_done = sem("silu_done")
        hidden_done = [sem("hidden_done0"), sem("hidden_done1")]
        h_hi_done = sem("h_hi_done")
        h_lo_done = [sem("h_lo_done0"), sem("h_lo_done1")]
        down_done = [sem("down_done0"), sem("down_done1")]
        summed = [sem("summed0"), sem("summed1")]
        stored = sem("stored")

        def rows_of(m, size):
            return (size, E) if m < 2 else (P, C * size)

        def per_block(table, r, v, size):
            m, ahead = UNIT[v]
            rows, cols = rows_of(m, size)
            if size == P:
                part = table[:].rearrange("p t m b -> p (t m b)")[:, bass.ds((r * 2 + ahead) * (3 * NB) + m * NB, NB)]
            else:
                part = table[0:rows, r * 2 + ahead, m, 0:NB] if m < 2 else table[:, r * 2 + ahead, m, 0::P // size]
            return part.unsqueeze(2).to_broadcast([rows, cols // BLOCK, BLOCK])

        def rounds(eng, body):
            with eng.Fori(0, ROUNDS - 2) as r:
                body(r, (P, P, P, P))
            body(ROUNDS - 2, (P, P, P, REST))
            body(ROUNDS - 1, (P, REST, 0, 0))

        def size_of(v, sizes):
            return sizes[UNIT[v][1]] if v < len(UNIT) else 0

        def ring(v, k):
            return (LEVELS * v + k) % SIGN_RING

        def split_parts(w12T, w3T, m, par, h, size):
            if m < 2:
                return (w12T[:, par, m, 4 * h:4 * h + 4, 0:size],
                        bank[:, TURN + h].rearrange("p (c s) -> p c s", s=P)[:, :, 0:size])
            return w3T[0:size, par, h * BANK:(h + 1) * BANK], bank[0:size, TURN + h]

        block = mine.enter_context(nc.Block())

        @block.sync
        def _(sp):
            def load(r, v, size):
                m, ahead = UNIT[v]
                rows, cols = rows_of(m, size)
                unit, slot = r * 6 + v, v % 2
                first = (r * 2 + ahead) * P
                if v >= 2:
                    sp.wait_ge(sign_set, (unit - 1) * LEVELS)
                    if m == 2:
                        sp.sem_inc(held, 1)
                if m < 2:
                    sp.dma_start(w_nat[0:rows, slot], (w1, w2)[m][bass.ds(first, rows), :]).then_inc(w_in[slot], 16)
                else:
                    sp.dma_start(w_nat[:, slot, 0:cols].rearrange("p (t h) -> p t h", t=C),
                                 w3.rearrange("(t p) h -> p t h", p=P)[:, :, bass.ds(first, size)]).then_inc(w_in[slot], 16)

            def body(r, sizes):
                for w in range(WINDOWS):
                    if size_of(AHEAD + w, sizes):
                        load(r, AHEAD + w, size_of(AHEAD + w, sizes))

            for v in range(AHEAD):
                load(0, v, P)
            rounds(sp, body)
            for st in range(T):
                for h in range(HALVES):
                    sp.wait_ge(summed[h], (ROUNDS - 1) * T + st + 1)
                sp.dma_start(out_dram[st * P:(st + 1) * P, :], acc[:, st]).then_inc(stored, 16)
            sp.wait_ge(stored, 16 * T)

        @block.gpsimd
        def _(pool):
            def divide(r, v, size):
                m, _ = UNIT[v]
                rows, cols = rows_of(m, size)
                slot = v % 2
                pool.wait_ge(w_in[slot], (r * 3 + v // 2 + 1) * 16)
                part = w_nat[0:rows, slot, 0:cols].rearrange("p (b e) -> p b e", e=BLOCK)
                nc.gpsimd.tensor_tensor(part, part, per_block(inv_absmax, r, v, size), ALU.mult).then_inc(divided, 1)

            def times_absmax(r, v, size):
                rows, cols = rows_of(UNIT[v][0], size)
                pool.wait_ge(sign_used, (r * 6 + v + 1) * LEVELS + SIGN_RING)
                part = codes[0:rows, v % 2, 0:cols].rearrange("p (b e) -> p b e", e=BLOCK)
                nc.gpsimd.tensor_tensor(part, part, per_block(absmax, r, v, size), ALU.mult).then_inc(rounded, 1)

            def hidden_lo(r, p, sb_, rows):
                tile, par = r * 2 + p, sb_ % 2
                cols = slice(sb_ * BANK, (sb_ + 1) * BANK)
                pool.wait_ge(h_hi_done, tile * SB + sb_ + 1)
                nc.gpsimd.tensor_tensor(hT_lo[0:rows, p, cols], hidden[0:rows, par], hT_hi[0:rows, p, cols],
                                        ALU.subtract).then_inc(h_lo_done[par], 1)

            def body(r, sizes):
                for w in range(WINDOWS):
                    v = AHEAD + w
                    if w + 1 < WINDOWS and size_of(v + 1, sizes):
                        divide(r, v + 1, size_of(v + 1, sizes))
                    elif w + 1 == WINDOWS and sizes[3]:
                        divide(r + 1, AHEAD, sizes[3])
                    if w < 4:
                        hidden_lo(r, w // 2, w % 2 * 2, sizes[w // 2])
                        hidden_lo(r, w // 2, w % 2 * 2 + 1, sizes[w // 2])
                    if size_of(v, sizes):
                        times_absmax(r, v, size_of(v, sizes))

            divide(0, 0, P)
            for v in range(AHEAD):
                divide(0, v + 1, P)
                times_absmax(0, v, P)
            rounds(pool, body)

        @block.scalar
        def _(act):
            def compare(r, v, size, ks):
                rows, cols = rows_of(UNIT[v][0], size)
                unit = r * 6 + v
                act.wait_ge(divided, unit + 1)
                for k in ks:
                    act.wait_ge(sign_used, unit * LEVELS + k + 1)
                    nc.scalar.activation(signs[0:rows, ring(v, k), 0:cols], w_nat[0:rows, v % 2, 0:cols], ACT.Sign,
                                         scale=COMPARE[k][0], bias=compare_bias[0:rows, k:k + 1]).then_inc(sign_set, 1)

            def turned_hi(r, v, size):
                m, ahead = UNIT[v]
                par = ahead % 2
                for h in range(HALVES):
                    act.wait_ge(w_turned, (r * 6 + v) * HALVES + h + 1)
                    dst, src = split_parts(w12T_hi, w3T_hi, m, par, h, size)
                    nc.scalar.activation(dst, src, ACT.Copy).then_inc(w_hi_done, 1)

            def silu(r, p, sb_, rows):
                tile, par = r * 2 + p, sb_ % 2
                act.wait_ge(gate_done, tile * SB + sb_ + 1)
                act.wait_ge(h_lo_done[par], tile * 2 + sb_ // 2)
                nc.scalar.activation(hidden[0:rows, par], bank[0:rows, GATE + par], ACT.Silu,
                                     scale=un_scale[0:rows, 0:1]).then_inc(silu_done, 1)

            def hidden_hi(r, p, sb_, rows):
                tile, par = r * 2 + p, sb_ % 2
                act.wait_ge(hidden_done[par], tile * 2 + sb_ // 2 + 1)
                nc.scalar.activation(hT_hi[0:rows, p, sb_ * BANK:(sb_ + 1) * BANK], hidden[0:rows, par], ACT.Copy).then_inc(h_hi_done, 1)

            def body(r, sizes):
                for w in range(WINDOWS):
                    v = AHEAD + w
                    size, turn = size_of(v, sizes), size_of(v - 1, sizes)
                    if size:
                        compare(r, v, size, range(0, LEVELS // 2 + 1))
                    if w < 4:
                        silu(r, w // 2, w % 2 * 2, sizes[w // 2])
                    if turn:
                        turned_hi(r, v - 1, turn)
                    if w < 4:
                        hidden_hi(r, w // 2, w % 2 * 2, sizes[w // 2])
                    if size:
                        compare(r, v, size, range(LEVELS // 2 + 1, LEVELS))
                    if w < 4:
                        silu(r, w // 2, w % 2 * 2 + 1, sizes[w // 2])
                        hidden_hi(r, w // 2, w % 2 * 2 + 1, sizes[w // 2])

            compare(0, 0, P, range(LEVELS))
            compare(0, 1, P, range(LEVELS))
            turned_hi(0, 0, P)
            turned_hi(0, 1, P)
            compare(0, 2, P, range(LEVELS))
            rounds(act, body)

        @block.vector
        def _(dve):
            V = nc.vector

            def sum_steps(r, v, size, ks):
                rows, cols = rows_of(UNIT[v][0], size)
                unit = r * 6 + v
                total = codes[0:rows, v % 2, 0:cols]
                for k in ks:
                    dve.wait_ge(sign_set, unit * LEVELS + k + 1)
                    part = signs[0:rows, ring(v, k), 0:cols]
                    if k == 0:
                        if v >= 2:
                            dve.wait_ge(w_turned, (unit - 1) * HALVES)
                        V.tensor_scalar(total, part, HALF_STEP[0], None, ALU.mult).then_inc(sign_used, 1)
                    else:
                        dve.wait_ge(sign_used, unit * LEVELS + SIGN_RING + k)
                        V.scalar_tensor_tensor(total, part, HALF_STEP[k], total, ALU.mult, ALU.add).then_inc(sign_used, 1)

            def turned_lo(r, v, size):
                m, ahead = UNIT[v]
                par = ahead % 2
                for h in range(HALVES):
                    dve.wait_ge(w_hi_done, (r * 6 + v) * HALVES + h + 1)
                    hi, src = split_parts(w12T_hi, w3T_hi, m, par, h, size)
                    lo, _ = split_parts(w12T_lo, w3T_lo, m, par, h, size)
                    V.tensor_tensor(lo, src, hi, ALU.subtract).then_inc(w_lo_done, 1)

            def hidden_value(r, p, sb_, rows):
                tile, par = r * 2 + p, sb_ % 2
                dve.wait_ge(silu_done, tile * SB + sb_ + 1)
                dve.wait_ge(up_done, tile * SB + sb_ + 1)
                V.scalar_tensor_tensor(hidden[0:rows, par], bank[0:rows, UP + par], un_scale[0:rows, 1:2], hidden[0:rows, par],
                                       ALU.mult, ALU.mult).then_inc(hidden_done[par], 1)

            def add_down(r, st, h):
                cols = slice(h * BANK, (h + 1) * BANK)
                dve.wait_ge(down_done[h], r * T + st + 1)
                V.scalar_tensor_tensor(acc[:, st, cols], bank[:, DOWN + h], un_scale[:, 2:3], acc[:, st, cols],
                                       ALU.mult, ALU.add).then_inc(summed[h], 1)

            def body(r, sizes):
                for w in range(WINDOWS):
                    v = AHEAD + w
                    size, turn = size_of(v, sizes), size_of(v - 1, sizes)
                    if w < 4:
                        if size:
                            sum_steps(r, v, size, range(0, LEVELS // 2))
                        hidden_value(r, w // 2, w % 2 * 2, sizes[w // 2])
                        if turn:
                            turned_lo(r, v - 1, turn)
                        if size:
                            sum_steps(r, v, size, range(LEVELS // 2, LEVELS))
                        hidden_value(r, w // 2, w % 2 * 2 + 1, sizes[w // 2])
                        continue
                    tiles = T // 2
                    for i in range(tiles):
                        st = (w - 4) * tiles + i
                        add_down(r, st, 0)
                        if size:
                            sum_steps(r, v, size, range(i * LEVELS // tiles, (i + 1) * LEVELS // tiles))
                        add_down(r, st, 1)
                        if i == tiles // 2 - 1 and turn:
                            turned_lo(r, v - 1, turn)

            dve.sem_inc(sign_used, SIGN_RING)
            sum_steps(0, 0, P, range(LEVELS))
            sum_steps(0, 1, P, range(LEVELS))
            turned_lo(0, 0, P)
            turned_lo(0, 1, P)
            sum_steps(0, 2, P, range(LEVELS))
            rounds(dve, body)

        @block.tensor
        def _(pe):
            def turn(r, v, size):
                m, _ = UNIT[v]
                unit, slot = r * 6 + v, v % 2
                pe.wait_ge(rounded, unit + 1)
                pe.wait_ge(w_lo_done, unit * HALVES)
                for h in range(HALVES):
                    for c in range(4 * h, 4 * h + 4):
                        if m < 2:
                            last = nc.tensor.transpose(bank[:, TURN + h, c % 4 * P:c % 4 * P + size],
                                                       codes[0:size, slot, c * P:(c + 1) * P], ident[0:size, 0:size])
                        else:
                            last = nc.tensor.transpose(bank[0:size, TURN + h, c % 4 * P:(c % 4 + 1) * P],
                                                       codes[:, slot, c * size:(c + 1) * size], ident[:])
                    last.then_inc(w_turned, 1)

            def gate_up(r, p, sb_, rows):
                tile, par = r * 2 + p, sb_ % 2
                cols = slice(sb_ * BANK, (sb_ + 1) * BANK)
                pe.wait_ge(hidden_done[par], tile * 2 + sb_ // 2)
                for m, to, done in ((0, GATE, gate_done), (1, UP, up_done)):
                    if sb_ == 0:
                        pe.wait_ge(w_lo_done, (r * 6 + 2 * p + m + 1) * HALVES)
                    dst = bank[0:rows, to + par]
                    for c in range(C):
                        hi, lo = w12T_hi[:, p, m, c, 0:rows], w12T_lo[:, p, m, c, 0:rows]
                        nc.tensor.matmul(dst, hi, x2T_hi[:, c, cols], start=c == 0, stop=False)
                        nc.tensor.matmul(dst, hi, x2T_lo[:, c, cols], start=False, stop=False)
                        last = nc.tensor.matmul(dst, lo, x2T_hi[:, c, cols], start=False, stop=c == C - 1)
                    last.then_inc(done, 1)

            def down(r, st, rows):
                toks = slice(st * P, (st + 1) * P)
                if st % ST_BLOCK == 0:
                    sb_ = st // ST_BLOCK
                    pe.wait_ge(h_lo_done[sb_ % 2], (r * 2 + 1) * 2 + sb_ // 2 + 1)
                for h in range(HALVES):
                    cols = slice(h * BANK, (h + 1) * BANK)
                    pe.wait_ge(summed[h], r * T + st)
                    for p in range(GROUP):
                        k = slice(0, rows[p])
                        dst = bank[:, DOWN + h]
                        nc.tensor.matmul(dst, hT_hi[k, p, toks], w3T_hi[k, p, cols], start=p == 0, stop=False)
                        nc.tensor.matmul(dst, hT_hi[k, p, toks], w3T_lo[k, p, cols], start=False, stop=False)
                        last = nc.tensor.matmul(dst, hT_lo[k, p, toks], w3T_hi[k, p, cols], start=False, stop=p == GROUP - 1)
                    last.then_inc(down_done[h], 1)

            def body(r, sizes):
                for w in range(WINDOWS):
                    v = AHEAD - 1 + w
                    size = size_of(v, sizes)
                    if w < 4:
                        gate_up(r, w // 2, w % 2 * 2, sizes[w // 2])
                        if size:
                            turn(r, v, size)
                        gate_up(r, w // 2, w % 2 * 2 + 1, sizes[w // 2])
                        continue
                    if w == 4:
                        pe.wait_ge(w_lo_done, (r * 6 + 6) * HALVES)
                    for i in range(T // 2):
                        down(r, (w - 4) * (T // 2) + i, sizes[0:GROUP])
                        if i == T // 4 - 1 and size:
                            turn(r, v, size)

            turn(0, 0, P)
            turn(0, 1, P)
            rounds(pe, body)


_INS = ["L0_attn_hidden_states", "L0_attn_wq", "L0_attn_bq", "L0_attn_wk", "L0_attn_bk", "L0_attn_wv", "L0_attn_bv",
        "L0_ffn_w1", "L0_ffn_w2", "L0_ffn_w3"]


def kernel(**inputs):
    import concourse.bacc as bacc
    from concourse.bass_utils import run_bass_kernel_spmd

    nc = bacc.Bacc("TRN2", target_bir_lowering=False, num_devices=1)
    arrays, args = {}, []
    for name in _INS:
        a = np.ascontiguousarray(inputs[name])
        arrays[f"in_{name}"] = a
        args.append(nc.dram_tensor(f"in_{name}", a.shape, mybir.dt.from_np(a.dtype), kind="ExternalInput").ap())
    shape = arrays["in_L0_attn_hidden_states"].shape
    out = nc.dram_tensor("out", shape, F32, kind="ExternalOutput").ap()
    layer(nc, *args, out)
    r = run_bass_kernel_spmd(nc, [arrays], core_ids=[0])
    return r.results[0]["out"]
```

```python
from contextlib import ExitStack

import numpy as np

import concourse.bass as bass
from concourse import mybir

F32 = mybir.dt.float32
F16 = mybir.dt.float16
I32 = mybir.dt.int32
I8 = mybir.dt.int8
ALU = mybir.AluOpType
ACT = mybir.ActivationFunctionType
AX = mybir.AxisListType
ALL_MAX = bass.bass_isa.ReduceOp.max

P = 128
QUAD = 32
BANK = 512
EPS = 1e-5
X_SCALE = 2.0 ** 10
TINY = 2.0 ** -60
EXPONENT_BITS = 0x7F800000
BLOCK = 64

NF4 = np.array([-1.0, -0.6961928009986877, -0.5250730514526367, -0.39491748809814453,
                -0.28444138169288635, -0.18477343022823334, -0.09105003625154495, 0.0,
                0.07958029955625534, 0.16093020141124725, 0.24611230194568634,
                0.33791524171829224, 0.44070982933044434, 0.5626170039176941,
                0.7229568362236023, 1.0], dtype=np.float32)
LEVELS = len(NF4) - 1
BOUNDS = (NF4[:-1] + NF4[1:]) * np.float32(0.5)


def strict_compare(bound):
    b = np.float64(bound)
    middle = (b + np.float64(np.nextafter(bound, np.float32(2.0)))) / 2
    best = None
    for k in range(2000):
        scale = np.float32(1.0 + k * 2.0 ** -23)
        bias = np.float32(np.float64(scale) * middle)
        off = abs(np.float64(bias) / np.float64(scale) - middle)
        if best is None or off < best[0]:
            best = (off, float(scale), -float(bias))
    return best[1], best[2]


COMPARE = [strict_compare(b) for b in BOUNDS]
GRID = 2.0 ** 25
HALF_STEP = [float(np.round((np.float64(NF4[i + 1]) - np.float64(NF4[i])) / 2 * GRID) / GRID)
             for i in range(LEVELS)]
SIGN_RING = 5



class Count:

    def __init__(self, sem):
        self.sem, self.base, self.off = sem, 0, 0

    def at(self, base):
        self.base, self.off = base, 0

    def mark(self, ins):
        self.off += 1
        return ins.then_inc(self.sem, 1)

    def wait(self, eng):
        eng.wait_ge(self.sem, self.base + self.off)


def layer(nc, x, wq, bq, wk, bk, wv, bv, w1, w2, w3, out):
    TOK, E = x.shape[-2:]
    FF = w1.shape[0]
    HD = QUAD
    HEADS = E // HD
    C = E // P
    T = TOK // P
    SB = TOK // BANK
    FT = FF // P
    REST = FF - FT * P
    NB = E // BLOCK
    HALVES = E // BANK
    GROUP = 2
    UNITS = 3 * (FT + 1)
    x_dram = x.rearrange("a s e -> (a s) e")
    x1_dram = nc.dram_tensor("x1", [TOK, E], F32).ap()
    x2_hi_dram = nc.dram_tensor("x2_hi_dram", [TOK, E], F16).ap()
    x2_lo_dram = nc.dram_tensor("x2_lo_dram", [TOK, E], F16).ap()

    with ExitStack() as whole:
        def sem(name):
            return whole.enter_context(nc.semaphore(name))

        def keep(name, shape, dt=F32):
            return whole.enter_context(nc.sbuf_tensor(name, shape, dt))

        bank = whole.enter_context(nc.psum_tensor("bank", [P, 8, BANK], F32))

        ident = keep("ident", [P, P])
        compare_bias = keep("compare_bias", [P, LEVELS])
        power = keep("power", [P, 2])
        absmax = keep("absmax", [P, FT + 1, 3, NB])
        top = keep("top", [P, 4])
        top_all = keep("top_all", [P, 4])
        pow2 = keep("pow2", [P, 4])
        inv_pow2 = keep("inv_pow2", [P, 4])
        w_scale = keep("w_scale", [P, 4])
        un_scale = keep("un_scale", [P, 4])
        stats = keep("stats", [P, 2, 6])
        mean_var = keep("mean_var", [P, 2])
        var_eps = keep("var_eps", [P, 1])
        rstd = keep("rstd", [P, 1])
        row_max = keep("row_max", [P, QUAD])
        row_sum = keep("row_sum", [P, QUAD])
        inv_sum = keep("inv_sum", [P, QUAD])

        consts_set = sem("consts_set")
        dve_seq = sem("dve_seq")

        attention(nc, locals())
        feed_forward(nc, locals())


def attention(nc, g):
    C, T, E, NB, FT, REST, HEADS, HD, HALVES = (g[k] for k in "C T E NB FT REST HEADS HD HALVES".split())
    bank, ident, sem = g["bank"], g["ident"], g["sem"]
    top, top_all, pow2, inv_pow2, w_scale, un_scale = (g[k] for k in "top top_all pow2 inv_pow2 w_scale un_scale".split())
    stats, mean_var, var_eps, rstd = (g[k] for k in "stats mean_var var_eps rstd".split())
    row_max, row_sum, inv_sum, absmax = (g[k] for k in "row_max row_sum inv_sum absmax".split())
    power, compare_bias, consts_set, dve_seq = (g[k] for k in "power compare_bias consts_set dve_seq".split())
    x_dram, x1_dram, x2_hi_dram, x2_lo_dram = (g[k] for k in "x_dram x1_dram x2_hi_dram x2_lo_dram".split())
    w_qkv = [g["wq"], g["wk"], g["wv"]]
    b_qkv = [g["bq"], g["bk"], g["bv"]]
    w1, w2, w3 = g["w1"], g["w2"], g["w3"]
    seq = Count(dve_seq)

    with ExitStack() as mine:
        def sb(name, shape, dt=F32):
            return mine.enter_context(nc.sbuf_tensor(name, shape, dt))

        wT_hi = sb("wT_hi", [P, C, 3, E], F16)
        wT_lo = sb("wT_lo", [P, C, 3, E], F16)

        w_in = [sem(f"w_in{m}") for m in range(3)]
        local_max = sem("local_max")
        global_max = sem("global_max")
        scale_set = sem("scale_set")
        w_turned = sem("w_turned")
        w_hi_done = sem("w_hi_done")
        w_lo_done = sem("w_lo_done")

        RING = 4
        FILLS = C * 2
        with nc.sbuf_tensor("w_raw", [P, 3, C, E], F32) as w_raw, nc.Block() as block:

            @block.sync
            def _(sp):
                for m in range(3):
                    sp.dma_start(w_raw[:, m], w_qkv[m].rearrange("(t p) d -> p t d", p=P)).then_inc(w_in[m], 16)

            @block.gpsimd
            def _(pool):
                pool.memset(ident[:], 0.0).then_inc(consts_set, 1)
                pool.memset(absmax[:], 0.0).then_inc(consts_set, 1)
                pool.memset(power[:, 0:1], -0.5).then_inc(consts_set, 1)
                pool.memset(power[:, 1:2], 0.5).then_inc(consts_set, 1)
                for i in range(LEVELS):
                    pool.memset(compare_bias[:, i:i + 1], COMPARE[i][1]).then_inc(consts_set, 1)
                pool.wait_ge(consts_set, 1)
                pool.affine_select(out=ident[:], in_=ident[:], compare_op=ALU.not_equal, fill=1.0, base=0,
                                   pattern=[[-1, P]], channel_multiplier=1).then_inc(consts_set, 1)
                for m in range(3):
                    pool.wait_ge(local_max, m + 1)
                    nc.gpsimd.partition_all_reduce(top_all[:, m:m + 1], top[:, m:m + 1], P, ALL_MAX).then_inc(global_max, 1)

            @block.vector
            def _(dve):
                for m in range(3):
                    col = slice(m, m + 1)
                    dve.wait_ge(w_in[m], 16)
                    nc.vector.tensor_reduce(top[:, col], w_raw[:, m].rearrange("p t d -> p (t d)"), AX.X, ALU.max,
                                            apply_absolute_value=True).then_inc(local_max, 1)
                    dve.wait_ge(global_max, m + 1)
                    seq.mark(nc.vector.tensor_scalar(pow2[:, col], top_all[:, col], TINY, None, ALU.max))
                    seq.wait(dve)
                    seq.mark(nc.vector.tensor_scalar(pow2[:, col].bitcast(I32), pow2[:, col].bitcast(I32),
                                                     EXPONENT_BITS, None, ALU.bitwise_and))
                    seq.wait(dve)
                    seq.mark(nc.vector.reciprocal(inv_pow2[:, col], pow2[:, col]))
                    seq.mark(nc.vector.tensor_scalar(un_scale[:, col], pow2[:, col], 2.0 ** -14 / X_SCALE, None, ALU.mult))
                    seq.wait(dve)
                    nc.vector.tensor_scalar(w_scale[:, col], inv_pow2[:, col], 2.0 ** 14, None, ALU.mult).then_inc(scale_set, 1)
                    dve.wait_ge(scale_set, m + 1)
                    for f in range(FILLS):
                        n = m * FILLS + f
                        c, half = f // 2, f % 2
                        dst = (slice(None), c, m, slice(half * BANK, half * BANK + BANK))
                        dve.wait_ge(w_hi_done, n + 1)
                        nc.vector.scalar_tensor_tensor(wT_lo[dst], bank[:, n % RING], w_scale[:, col], wT_hi[dst],
                                                       ALU.mult, ALU.subtract).then_inc(w_lo_done, 1)

            @block.scalar
            def _(act):
                for m in range(3):
                    act.wait_ge(scale_set, m + 1)
                    for f in range(FILLS):
                        n = m * FILLS + f
                        c, half = f // 2, f % 2
                        act.wait_ge(w_turned, n + 1)
                        nc.scalar.activation(wT_hi[:, c, m, half * BANK:half * BANK + BANK], bank[:, n % RING],
                                             ACT.Copy, scale=w_scale[:, m:m + 1]).then_inc(w_hi_done, 1)

            @block.tensor
            def _(pe):
                pe.wait_ge(consts_set, 5 + LEVELS)
                for m in range(3):
                    pe.wait_ge(w_in[m], 16)
                    for f in range(FILLS):
                        n = m * FILLS + f
                        c, half = f // 2, f % 2
                        if n >= RING:
                            pe.wait_ge(w_lo_done, n - RING + 1)
                        for j in range(BANK // P):
                            t = half * (BANK // P) + j
                            last = nc.tensor.transpose(bank[:, n % RING, j * P:(j + 1) * P],
                                                       w_raw[:, m, t, c * P:(c + 1) * P], ident[:])
                        last.then_inc(w_turned, 1)

        bias = sb("bias", [P, 3, E])
        x_nat = sb("x_nat", [P, 2, E])
        x_res = sb("x_res", [P, E])
        xT_hi = sb("xT_hi", [P, 2, C, P], F16)
        xT_lo = sb("xT_lo", [P, 2, C, P], F16)
        x2_hi = sb("x2_hi", [P, C, P], F16)
        x2_lo = sb("x2_lo", [P, C, P], F16)
        qkv = sb("qkv", [P, 3, E])
        qT = sb("qT", [P, QUAD, HEADS])
        kT = sb("kT", [P, QUAD, HEADS])
        vT = sb("vT", [P, QUAD, HD])
        q_diag = sb("q_diag", [P, QUAD, P])
        p_diag = sb("p_diag", [P, QUAD, P])
        probs = sb("probs", [P, QUAD, HEADS])
        flipped = sb("flipped", [P, E])
        ff_raw = sb("ff_raw", [P, E])
        stats2 = sb("stats2", [P, 2, 6])
        mean_var2 = sb("mean_var2", [P, 2])
        var_eps2 = sb("var_eps2", [P, 1])
        rstd2 = sb("rstd2", [P, 1])

        bias_in = sem("bias_in")
        diag_zero = sem("diag_zero")
        x_in = [sem("x_in0"), sem("x_in1")]
        res_in = sem("res_in")
        var_ready = sem("var_ready")
        rstd_ready = sem("rstd_ready")
        normed = sem("normed")
        x_turned = sem("x_turned")
        x_hi_done = sem("x_hi_done")
        x_lo_done = sem("x_lo_done")
        projected = sem("projected")
        evacuated = sem("evacuated")
        q_ready = sem("q_ready")
        q_placed = sem("q_placed")
        k_ready = sem("k_ready")
        v_ready = sem("v_ready")
        scores_done = sem("scores_done")
        centered = sem("centered")
        exp_done = sem("exp_done")
        p_ready = sem("p_ready")
        p_placed = sem("p_placed")
        context_done = sem("context_done")
        ctx_ready = sem("ctx_ready")
        res_done = sem("res_done")
        x1_out = sem("x1_out")
        var2_ready = sem("var2_ready")
        rstd2_ready = sem("rstd2_ready")
        normed2 = sem("normed2")
        x2_turned = sem("x2_turned")
        x2_hi_done = sem("x2_hi_done")
        x2_lo_done = sem("x2_lo_done")
        x2_out = sem("x2_out")
        ff_in = sem("ff_in")
        held = sem("held")
        absmax_done = sem("absmax_done")

        PROJ_RING = 4
        mixing = bank[:, 4:6].rearrange("p b n -> p (b n)")
        scores = mixing.rearrange("p (t h) -> p t h", h=HEADS)
        context = mixing.rearrange("p (t d) -> p t d", d=HD)
        TURN = 6
        quadrants = [slice(a * QUAD, (a + 1) * QUAD) for a in range(P // QUAD)]

        LOOP = (T - 4) // 2
        MARKS = 8

        def all_steps(eng, step):
            step(0, 0, None, attend=False, end=False)
            step(1, 1, None, end=False)
            with eng.Fori(0, LOOP) as it:
                for u in range(2):
                    step(it * 2 + 2 + u, u, it)
            step(T - 2, 0, None)
            step(T - 1, 1, None, normalize=False)
            step(T, 0, None, project=False, normalize=False)
            step(T + 1, 1, None, project=False, normalize=False, attend=False)

        IN_LOOP = (5, 4)
        assert FT == 2 + 3 * LOOP + 1 and REST

        def looks(n, u, it):
            if it is not None:
                places = [u * IN_LOOP[0] + k for k in range(IN_LOOP[u])]
                return [(it * 3 + 2 + q // 3, q % 3, it * 9 + 6 + q, P) for q in places]
            tile = {0: 0, 1: 1, T - 2: FT - 1, T - 1: FT}.get(n)
            return [] if tile is None else [(tile, m, tile * 3 + m, P if tile < FT else REST) for m in range(3)]

        with nc.Block() as block:

            @block.sync
            def _(sp):
                def load_x(n, slot):
                    sp.dma_start(x_nat[:, slot], x_dram[bass.ds(n * P, P), :]).then_inc(x_in[slot], 16)

                def load_res(n):
                    sp.dma_start(x_res[:], x_dram[bass.ds(n * P, P), :]).then_inc(res_in, 16)

                def load_ff(tile, m, j, rows):
                    first = tile * P
                    sp.wait_ge(absmax_done, j + 1)
                    if m == 2:
                        sp.sem_inc(held, 1)
                    if m < 2:
                        sp.dma_start(ff_raw[0:rows], (w1, w2)[m][bass.ds(first, rows), :]).then_inc(ff_in, 16)
                    else:
                        sp.dma_start(ff_raw[:, 0:C * rows].rearrange("p (t h) -> p t h", t=C),
                                     w3.rearrange("(t p) h -> p t h", p=P)[:, :, bass.ds(first, rows)]).then_inc(ff_in, 16)

                def step(n, u, it, project=True, normalize=True, attend=True, end=True):
                    todo = looks(n, u, it)
                    if normalize and not (it is None and n + 2 >= T):
                        sp.wait_ge(x_turned, 2 * n + 2)
                        load_x(n + 2, u)
                    for look in todo[:1]:
                        load_ff(*look)
                    if end:
                        sp.wait_ge(res_done, n - 1)
                        sp.dma_start(x1_dram[bass.ds((n - 2) * P, P), :], x_res[:]).then_inc(x1_out, 16)
                    for look in todo[1:4]:
                        load_ff(*look)
                    if end and attend:
                        sp.wait_ge(x2_turned, 2 * (n - 1))
                        load_res(n - 1)
                    for look in todo[4:]:
                        load_ff(*look)
                    if end:
                        sp.wait_ge(x2_lo_done, 2 * n)
                        sp.sem_inc(held, 1)
                        for dram, part in ((x2_hi_dram, x2_hi), (x2_lo_dram, x2_lo)):
                            sp.dma_start(dram[bass.ds((n - 2) * P, P), :], part[:].rearrange("p c s -> p (c s)")).then_inc(x2_out, 16)

                sp.sem_inc(x2_out, 32)
                load_x(0, 0)
                load_x(1, 1)
                for m in range(3):
                    sp.dma_start(bias[:, m], b_qkv[m].rearrange("(o n) -> o n", o=1).to_broadcast([P, E])).then_inc(bias_in, 16)
                load_res(0)
                all_steps(sp, step)
                sp.wait_ge(x1_out, 16 * T)
                sp.wait_ge(x2_out, 32 * (T + 1))

            @block.gpsimd
            def _(pool):
                def step(n, u, it, project=True, normalize=True, attend=True, end=True):
                    if normalize:
                        inv_std(n + 1)
                    if end:
                        pool.wait_ge(ctx_ready, n - 1)
                        pool.wait_ge(res_in, 16 * (n - 1))
                        nc.gpsimd.tensor_tensor(x_res[:], x_res[:], flipped[:], ALU.add).then_inc(res_done, 1)
                        pool.wait_ge(var2_ready, n - 1)
                        nc.gpsimd.tensor_tensor(rstd2[:], var_eps2[:], power[:, 0:1], ALU.pow).then_inc(rstd2_ready, 1)

                def inv_std(n):
                    pool.wait_ge(var_ready, n + 1)
                    nc.gpsimd.tensor_tensor(rstd[:], var_eps[:], power[:, 0:1], ALU.pow).then_inc(rstd_ready, 1)

                inv_std(0)
                pool.memset(q_diag[:], 0.0).then_inc(diag_zero, 1)
                pool.memset(p_diag[:], 0.0).then_inc(diag_zero, 1)
                all_steps(pool, step)

            @block.vector
            def _(dve):
                def moments(rows, part, mv, ve, ready):
                    for h in range(2):
                        last = nc.vector.bn_stats(part[:, h], rows[:, h * BANK:(h + 1) * BANK])
                    seq.mark(last)
                    seq.wait(dve)
                    dve.sem_inc(held, 1)
                    seq.mark(nc.vector.bn_aggr(mv[:], part[:].rearrange("p h s -> p (h s)")))
                    seq.wait(dve)
                    nc.vector.tensor_scalar(ve[:], mv[:, 1:2], EPS, None, ALU.add).then_inc(ready, 1)

                def split_lo(n, lo, hi, hi_done, lo_done):
                    for h in range(2):
                        dve.wait_ge(hi_done, 2 * n + h + 1)
                        nc.vector.scalar_tensor_tensor(lo[:, 4 * h:4 * h + 4].rearrange("p c s -> p (c s)"), bank[:, TURN + h], X_SCALE,
                                                       hi[:, 4 * h:4 * h + 4].rearrange("p c s -> p (c s)"),
                                                       ALU.mult, ALU.subtract).then_inc(lo_done, 1)

                def norm_stats(n, slot, loaded):
                    dve.wait_ge(x_in[slot], 16 * loaded)
                    moments(x_nat[:, slot], stats, mean_var, var_eps, var_ready)

                def norm_apply(n, slot):
                    dve.wait_ge(rstd_ready, n + 1)
                    nc.vector.tensor_scalar(x_nat[:, slot], x_nat[:, slot], mean_var[:, 0:1], rstd[:, 0:1],
                                            ALU.subtract, ALU.mult).then_inc(normed, 1)

                def evacuate(n, u, m, h):
                    i = 2 * m + h
                    cols = slice(h * BANK, (h + 1) * BANK)
                    dve.wait_ge(projected, 6 * n + i + 1)
                    nc.vector.scalar_tensor_tensor(qkv[:, m, cols], bank[:, (6 * u + i) % PROJ_RING], un_scale[:, m:m + 1],
                                                   bias[:, m, cols], ALU.mult, ALU.add).then_inc(evacuated, 1)

                def look_at(tile, m, j, rows):
                    dve.wait_ge(ff_in, 16 * (j + 1))
                    if m < 2:
                        part, blocks = slice(0, rows), NB
                    else:
                        part, blocks = slice(0, P), C * rows // BLOCK
                    if rows == P:
                        to = absmax[:].rearrange("p t m b -> p (t m b)")[:, bass.ds(j * NB, NB)]
                    else:
                        to = absmax[part, tile, m, 0:NB] if m < 2 else absmax[:, tile, m, 0::P // rows]
                    nc.vector.tensor_reduce(to, ff_raw[part, 0:blocks * BLOCK].rearrange("p (b e) -> p b e", e=BLOCK),
                                            AX.X, ALU.max, apply_absolute_value=True).then_inc(absmax_done, 1)

                def step(n, u, it, project=True, normalize=True, attend=True, end=True):
                    todo = looks(n, u, it)

                    def look():
                        if todo:
                            look_at(*todo.pop(0))

                    if it is not None:
                        seq.at(before_loop + it * (2 * MARKS) + u * MARKS)
                    if end:
                        dve.wait_ge(context_done, n - 1)
                        seq.wait(dve)
                        seq.mark(nc.vector.tensor_tensor(probs[:], context, inv_sum[:].unsqueeze(2).to_broadcast([P, QUAD, HD]),
                                                         ALU.mult))
                        seq.wait(dve)
                        nc.vector.transpose(flipped[:].rearrange("p (h d) -> p d h", d=HD),
                                            probs[:].rearrange("p t d -> p d t")).then_inc(ctx_ready, 1)
                    if attend:
                        evacuate(n - 1, 1 - u, 2, 1)
                        dve.wait_ge(evacuated, 6 * n)
                        nc.vector.transpose(vT[:].rearrange("p t d -> p d t"),
                                            qkv[:, 2].rearrange("p (h d) -> p d h", d=HD)).then_inc(v_ready, 1)
                    if normalize:
                        norm_apply(n + 1, 1 - u)
                    look()
                    if end:
                        dve.wait_ge(res_done, n - 1)
                        moments(x_res[:], stats2, mean_var2, var_eps2, var2_ready)
                    if project:
                        evacuate(n, u, 0, 0)
                    look()
                    if project:
                        evacuate(n, u, 0, 1)
                        dve.wait_ge(evacuated, 6 * n + 2)
                        if not (it is None and n == 0):
                            dve.wait_ge(q_placed, n)
                        nc.vector.transpose(qT[:].rearrange("p t h -> p h t"),
                                            qkv[:, 0].rearrange("p (h d) -> p h d", d=HD)).then_inc(q_ready, 1)
                    if end:
                        dve.wait_ge(rstd2_ready, n - 1)
                        dve.wait_ge(x1_out, 16 * (n - 1))
                        nc.vector.tensor_scalar(x_res[:], x_res[:], mean_var2[:, 0:1], rstd2[:, 0:1],
                                                ALU.subtract, ALU.mult).then_inc(normed2, 1)
                    if attend:
                        dve.wait_ge(scores_done, n)
                        seq.mark(nc.vector.tensor_reduce(row_max[:], scores, AX.X, ALU.max))
                        seq.wait(dve)
                        nc.vector.tensor_tensor(probs[:], scores, row_max[:].unsqueeze(2).to_broadcast([P, QUAD, HEADS]),
                                                ALU.subtract).then_inc(centered, 1)
                    look()
                    if normalize:
                        split_lo(n + 1, xT_lo[:, 1 - u], xT_hi[:, 1 - u], x_hi_done, x_lo_done)
                    if attend:
                        dve.wait_ge(exp_done, n)
                        seq.mark(nc.vector.tensor_reduce(row_sum[:], probs[:], AX.X, ALU.add))
                        seq.wait(dve)
                        seq.mark(nc.vector.reciprocal(inv_sum[:], row_sum[:]))
                        if end:
                            dve.wait_ge(res_done, n - 1)
                        nc.vector.transpose(flipped[:].rearrange("p (t h) -> p t h", h=HEADS), probs[:]).then_inc(p_ready, 1)
                    if project:
                        evacuate(n, u, 1, 0)
                    look()
                    if project:
                        evacuate(n, u, 1, 1)
                        dve.wait_ge(evacuated, 6 * n + 4)
                        nc.vector.transpose(kT[:].rearrange("p t h -> p h t"),
                                            qkv[:, 1].rearrange("p (h d) -> p h d", d=HD)).then_inc(k_ready, 1)
                    if end:
                        split_lo(n - 2, x2_lo, x2_hi, x2_hi_done, x2_lo_done)
                    look()
                    if project:
                        evacuate(n, u, 2, 0)
                    if it is not None or n + 2 < T:
                        norm_stats(n + 2, u, n // 2 + 2 if it is None else it + 3)
                    if it is not None:
                        assert seq.off == MARKS
                        if u == 1:
                            seq.at(before_loop + LOOP * 2 * MARKS)

                before_loop = 3 * 4 + 2 * 2 + 2 + 5
                dve.sem_inc(absmax_done, 1)
                dve.sem_inc(x2_lo_done, 2)
                dve.wait_ge(consts_set, 5 + LEVELS)
                seq.at(3 * 4)
                norm_stats(0, 0, 1)
                norm_apply(0, 0)
                split_lo(0, xT_lo[:, 0], xT_hi[:, 0], x_hi_done, x_lo_done)
                norm_stats(1, 1, 1)
                dve.wait_ge(bias_in, 48)
                all_steps(dve, step)
                dve.wait_ge(absmax_done, 3 * FT + 3 + 1)

            @block.scalar
            def _(act):
                def split_hi(n, hi, turned, hi_done):
                    for h in range(2):
                        act.wait_ge(turned, 2 * n + h + 1)
                        nc.scalar.activation(hi[:, 4 * h:4 * h + 4].rearrange("p c s -> p (c s)"), bank[:, TURN + h],
                                             ACT.Copy, scale=X_SCALE).then_inc(hi_done, 1)

                def place(diag, compact, done):
                    for rows in quadrants:
                        last = nc.scalar.activation(diag[rows, :, rows], compact[rows].rearrange("p (t h) -> p t h", h=HEADS), ACT.Copy)
                    last.then_inc(done, 1)

                def step(n, u, it, project=True, normalize=True, attend=True, end=True):
                    if attend:
                        act.wait_ge(centered, n)
                        flat = probs[:].rearrange("p t h -> p (t h)")
                        nc.scalar.activation(flat, flat, ACT.Exp, scale=float(1 / np.sqrt(np.float32(HD)))).then_inc(exp_done, 1)
                    if normalize:
                        split_hi(n + 1, xT_hi[:, 1 - u], x_turned, x_hi_done)
                    if attend:
                        act.wait_ge(p_ready, n)
                        if end:
                            act.wait_ge(context_done, n - 1)
                        place(p_diag, flipped[:], p_placed)
                    if end:
                        act.wait_ge(x2_out, 32 * (n - 1))
                        split_hi(n - 2, x2_hi, x2_turned, x2_hi_done)
                    if project:
                        act.wait_ge(q_ready, n + 1)
                        if attend:
                            act.wait_ge(scores_done, n)
                        place(q_diag, qT[:].rearrange("p t h -> p (t h)"), q_placed)

                split_hi(0, xT_hi[:, 0], x_turned, x_hi_done)
                act.wait_ge(diag_zero, 2)
                all_steps(act, step)

            @block.tensor
            def _(pe):
                def turn(rows, done):
                    for h in range(2):
                        for c in range(4 * h, 4 * h + 4):
                            last = nc.tensor.transpose(bank[:, TURN + h, (c % 4) * P:(c % 4 + 1) * P], rows[:, c * P:(c + 1) * P], ident[:])
                        last.then_inc(done, 1)

                def project_one(n, u, it, m, between=None):
                    for h in range(2):
                        i = 2 * m + h
                        to = bank[:, (6 * u + i) % PROJ_RING]
                        cols = slice(h * BANK, (h + 1) * BANK)
                        if not (it is None and n == 0 and i < PROJ_RING):
                            pe.wait_ge(evacuated, 6 * n + i + 1 - PROJ_RING)
                        passes = [(x, w) for c in range(C) for x, w in ((xT_hi[:, u, c], wT_hi[:, c, m, cols]),
                                                                        (xT_hi[:, u, c], wT_lo[:, c, m, cols]),
                                                                        (xT_lo[:, u, c], wT_hi[:, c, m, cols]))]
                        for j, (x, w) in enumerate(passes):
                            ins = nc.tensor.matmul(to, x, w, start=j == 0, stop=j == len(passes) - 1)
                            if j == len(passes) - 1:
                                ins.then_inc(projected, 1)
                            t = h * len(passes) + j - (2 * len(passes) - QUAD)
                            if between and t >= 0:
                                between(t, t + 1)

                def step(n, u, it, project=True, normalize=True, attend=True, end=True):
                    def score(first, last):
                        if first == 0:
                            pe.wait_ge(q_placed, n)
                            pe.wait_ge(k_ready, n)
                            if end:
                                pe.wait_ge(ctx_ready, n - 1)
                        for t in range(first, last):
                            ins = nc.tensor.matmul(scores[:, t], q_diag[:, t], kT[:, t], start=True, stop=True)
                        if last == QUAD:
                            ins.then_inc(scores_done, 1)

                    def mix(first, last):
                        if first == 0:
                            pe.wait_ge(p_placed, n)
                            pe.wait_ge(v_ready, n)
                        for t in range(first, last):
                            ins = nc.tensor.matmul(context[:, t], p_diag[:, t], vT[:, t], start=True, stop=True)
                        if last == QUAD:
                            ins.then_inc(context_done, 1)

                    if project:
                        pe.wait_ge(x_lo_done, 2 * n + 2)
                        project_one(n, u, it, 0, score if attend else None)
                    elif attend:
                        score(0, QUAD)
                    if normalize:
                        pe.wait_ge(normed, n + 2)
                        if end:
                            pe.wait_ge(x2_lo_done, 2 * (n - 1))
                        turn(x_nat[:, 1 - u], x_turned)
                    if project:
                        project_one(n, u, it, 1)
                    if end:
                        pe.wait_ge(normed2, n - 1)
                        if normalize:
                            pe.wait_ge(x_lo_done, 2 * (n + 2))
                        else:
                            pe.wait_ge(x2_lo_done, 2 * (n - 1))
                        turn(x_res[:], x2_turned)
                    if project:
                        project_one(n, u, it, 2, mix if attend else None)
                    elif attend:
                        mix(0, QUAD)

                pe.wait_ge(normed, 1)
                turn(x_nat[:, 0], x_turned)
                all_steps(pe, step)


def feed_forward(nc, g):
    C, T, E, NB, FT, REST, SB, HALVES, GROUP, UNITS = (g[k] for k in "C T E NB FT REST SB HALVES GROUP UNITS".split())
    bank, ident, sem = g["bank"], g["ident"], g["sem"]
    absmax, compare_bias, power = (g[k] for k in "absmax compare_bias power".split())
    top, top_all, pow2, inv_pow2, w_scale, un_scale = (g[k] for k in "top top_all pow2 inv_pow2 w_scale un_scale".split())
    x1_dram, x2_hi_dram, x2_lo_dram, out = (g[k] for k in "x1_dram x2_hi_dram x2_lo_dram out".split())
    w1, w2, w3 = g["w1"], g["w2"], g["w3"]
    out_dram = out.rearrange("a s e -> (a s) e")
    GATE, UP, TURN, DOWN = 0, 2, 4, 6
    ROUNDS = (FT + 1) // GROUP
    ST_BLOCK = BANK // P

    UNIT = ((0, 0), (1, 0), (0, 1), (1, 1), (2, 0), (2, 1), (0, 2), (1, 2), (0, 3))
    AHEAD = 3
    WINDOWS = 6
    STEP_STARTS = (0, 16, 32, 48, 64, 77, 6 * LEVELS)

    with ExitStack() as mine:
        def sb(name, shape, dt=F32):
            return mine.enter_context(nc.sbuf_tensor(name, shape, dt))

        acc = sb("acc", [P, T, E])
        x2T_hi = sb("x2T_hi", [P, T, C, P], F16)
        x2T_lo = sb("x2T_lo", [P, T, C, P], F16)
        inv_absmax = sb("inv_absmax", [P, FT + 1, 3, NB])
        w12T_hi = sb("w12T_hi", [P, 2, 2, C, P], F16)
        w12T_lo = sb("w12T_lo", [P, 2, 2, C, P], F16)
        w3T_hi = sb("w3T_hi", [P, 2, E], F16)
        w3T_lo = sb("w3T_lo", [P, 2, E], F16)
        hT_hi = sb("hT_hi", [P, 2, SB * BANK], F16)
        hT_lo = sb("hT_lo", [P, 2, SB * BANK], F16)
        w_nat = sb("w_nat", [P, 2, E])
        codes = sb("codes", [P, 2, E])
        signs = sb("signs", [P, SIGN_RING, E], I8)
        hidden = sb("hidden", [P, 2, BANK])
        down_part = sb("down_part", [P, 2, BANK])

        spare = codes[:, 1]
        squares = spare[:, 0:(FT + 1) * 2 * NB].rearrange("p (t m b) -> p t m b", m=2, b=NB)
        norms = spare[:, (FT + 1) * 2 * NB:][:, 0:(FT + 1) * 2].rearrange("p (t m) -> p t m", m=2)
        norm_prod = spare[:, (FT + 1) * 2 * (NB + 1):][:, 0:FT + 1]

        seq = Count(sem("scale_seq"))
        inv_ready = sem("inv_ready")
        ff_max = sem("ff_max")
        ff_max_all = sem("ff_max_all")
        ff_floor = sem("ff_floor")
        ff_root = sem("ff_root")
        scaled = sem("scaled")
        x2_in = [sem(f"x2_in{b}") for b in range(SB)]
        acc_in = sem("acc_in")
        w_in = [sem("ffw_in0"), sem("ffw_in1")]
        divided = sem("divided")
        held = sem("held3")
        sign_set = sem("sign_set")
        left_sum = sem("left_sum")
        sign_used = sem("sign_used")
        rounded = sem("rounded")
        w_turned = sem("ffw_turned")
        w_hi_done = sem("ffw_hi_done")
        w_lo_done = sem("ffw_lo_done")
        gate_done = sem("gate_done")
        up_done = sem("up_done")
        silu_done = sem("silu_done")
        hidden_done = [sem("hidden_done0"), sem("hidden_done1")]
        h_hi_done = sem("h_hi_done")
        h_lo_done = [sem("h_lo_done0"), sem("h_lo_done1")]
        down_read = [sem("down_read0"), sem("down_read1")]
        down_done = [sem("down_done0"), sem("down_done1")]
        summed = sem("summed")
        stored = sem("stored")

        def down_bank(st, h):
            return bank[:, (GATE, UP)[h]] if st % 2 == 0 else bank[:, DOWN + h]

        def rows_of(m, size):
            return (size, E) if m < 2 else (P, C * size)

        def per_block(table, r, v, size):
            m, ahead = UNIT[v]
            rows, cols = rows_of(m, size)
            if size == P:
                part = table[:].rearrange("p t m b -> p (t m b)")[:, bass.ds((r * 2 + ahead) * (3 * NB) + m * NB, NB)]
            else:
                part = table[0:rows, r * 2 + ahead, m, 0:NB] if m < 2 else table[:, r * 2 + ahead, m, 0::P // size]
            return part.unsqueeze(2).to_broadcast([rows, cols // BLOCK, BLOCK])

        def rounds(eng, body):
            with eng.Fori(0, ROUNDS - 2) as r:
                body(r, FULL)
            body(ROUNDS - 2, (P, P, P, REST))
            body(ROUNDS - 1, (P, REST, 0, 0))

        def size_of(v, sizes):
            return sizes[UNIT[v][1]] if v < len(UNIT) else 0

        def steps_of(w, sizes):
            steps = [divmod(at, LEVELS) for at in range(STEP_STARTS[w], STEP_STARTS[w + 1])]
            return [(AHEAD + v, k) for v, k in steps if size_of(AHEAD + v, sizes)]

        FULL = (P, P, P, P)
        first_units = [[(v, k) for k in range(LEVELS)] for v in range(AHEAD)]

        def portion(steps, i, n):
            return steps[i * len(steps) // n:(i + 1) * len(steps) // n]

        def ring(v, k):
            return (LEVELS * v + k) % SIGN_RING

        def split_parts(w12T, w3T, m, par, h, size):
            if m < 2:
                return (w12T[:, par, m, 4 * h:4 * h + 4, 0:size],
                        bank[:, TURN + h].rearrange("p (c s) -> p c s", s=P)[:, :, 0:size])
            return w3T[0:size, par, h * BANK:(h + 1) * BANK], bank[0:size, TURN + h]

        block = mine.enter_context(nc.Block())

        @block.sync
        def _(sp):
            def load(r, v, size):
                m, ahead = UNIT[v]
                rows, cols = rows_of(m, size)
                unit, slot = r * 6 + v, v % 2
                first = (r * 2 + ahead) * P
                if v >= 2:
                    sp.wait_ge(sign_set, (unit - 1) * LEVELS)
                    if m == 2:
                        sp.sem_inc(held, 1)
                if m < 2:
                    sp.dma_start(w_nat[0:rows, slot], (w1, w2)[m][bass.ds(first, rows), :]).then_inc(w_in[slot], 16)
                else:
                    sp.dma_start(w_nat[:, slot, 0:cols].rearrange("p (t h) -> p t h", t=C),
                                 w3.rearrange("(t p) h -> p t h", p=P)[:, :, bass.ds(first, size)]).then_inc(w_in[slot], 16)

            def body(r, sizes):
                for w in range(WINDOWS):
                    if size_of(AHEAD + w, sizes):
                        load(r, AHEAD + w, size_of(AHEAD + w, sizes))

            for v in range(2):
                load(0, v, P)
            for b in range(SB):
                tiles = slice(b * ST_BLOCK, (b + 1) * ST_BLOCK)
                for part, dram in ((x2T_hi, x2_hi_dram), (x2T_lo, x2_lo_dram)):
                    sp.dma_start(part[:, tiles].rearrange("p t c s -> p t (c s)"),
                                 dram.rearrange("(t p) f -> p t f", p=P)[:, tiles]).then_inc(x2_in[b], 16)
            load(0, 2, P)
            rounds(sp, body)
            for st in range(T):
                sp.wait_ge(down_read[0], (ROUNDS - 1) * T + st + 3)
                sp.wait_ge(summed, (ROUNDS - 1) * T + st + 1 + 2)
                sp.dma_start(out_dram[st * P:(st + 1) * P, :], acc[:, st]).then_inc(stored, 16)
            sp.wait_ge(stored, 16 * T)

        @block.gpsimd
        def _(pool):
            def divide(r, v, size):
                m, _ = UNIT[v]
                rows, cols = rows_of(m, size)
                slot = v % 2
                pool.wait_ge(w_in[slot], (r * 3 + v // 2 + 1) * 16)
                part = w_nat[0:rows, slot, 0:cols].rearrange("p (b e) -> p b e", e=BLOCK)
                nc.gpsimd.tensor_tensor(part, part, per_block(inv_absmax, r, v, size), ALU.mult).then_inc(divided, 1)

            def times_absmax(r, v, size):
                rows, cols = rows_of(UNIT[v][0], size)
                pool.wait_ge(sign_used, (r * 6 + v + 1) * LEVELS + SIGN_RING)
                part = codes[0:rows, v % 2, 0:cols].rearrange("p (b e) -> p b e", e=BLOCK)
                nc.gpsimd.tensor_tensor(part, part, per_block(absmax, r, v, size), ALU.mult).then_inc(rounded, 1)

            def hidden_lo(r, p, sb_, rows):
                tile, par = r * 2 + p, sb_ % 2
                cols = slice(sb_ * BANK, (sb_ + 1) * BANK)
                pool.wait_ge(h_hi_done, tile * SB + sb_ + 1)
                nc.gpsimd.tensor_tensor(hT_lo[0:rows, p, cols], hidden[0:rows, par], hT_hi[0:rows, p, cols],
                                        ALU.subtract).then_inc(h_lo_done[par], 1)

            def add_down(r, st):
                pool.wait_ge(acc_in, 16)
                pool.wait_ge(down_read[1], r * T + st + 3)
                nc.gpsimd.tensor_tensor(acc[:, st, BANK:], acc[:, st, BANK:], down_part[:, st % 2], ALU.add).then_inc(summed, 1)

            def body(r, sizes):
                for w in range(WINDOWS):
                    v = AHEAD + w
                    if w + 1 < WINDOWS and size_of(v + 1, sizes):
                        divide(r, v + 1, size_of(v + 1, sizes))
                    elif w + 1 == WINDOWS and sizes[3]:
                        divide(r + 1, AHEAD, sizes[3])
                    if w < 4:
                        hidden_lo(r, w // 2, w % 2 * 2, sizes[w // 2])
                        if size_of(v, sizes):
                            times_absmax(r, v, size_of(v, sizes))
                        hidden_lo(r, w // 2, w % 2 * 2 + 1, sizes[w // 2])
                    else:
                        for i in range(T // 2):
                            add_down(r, (w - 4) * (T // 2) + i)
                        if size_of(v, sizes):
                            times_absmax(r, v, size_of(v, sizes))

            pool.sem_inc(summed, 2)
            pool.wait_ge(ff_max, 1)
            nc.gpsimd.partition_all_reduce(top_all[:], top[:], P, ALL_MAX).then_inc(ff_max_all, 1)
            pool.wait_ge(inv_ready, 1)
            divide(0, 0, P)
            pool.wait_ge(ff_floor, 1)
            nc.gpsimd.tensor_tensor(top_all[:, 3:4], pow2[:, 3:4], power[:, 1:2], ALU.pow).then_inc(ff_root, 1)
            for v in range(AHEAD):
                divide(0, v + 1, P)
                if v == 0:
                    pool.wait_ge(scaled, 1)
                times_absmax(0, v, P)
            rounds(pool, body)

        @block.scalar
        def _(act):
            def compare(r, steps, sizes):
                for v, k in steps:
                    size = size_of(v, sizes)
                    rows, cols = rows_of(UNIT[v][0], size)
                    unit = r * 6 + v
                    if k == 0:
                        act.wait_ge(divided, unit + 1)
                    act.wait_ge(sign_used, unit * LEVELS + k + 1)
                    nc.scalar.activation(signs[0:rows, ring(v, k), 0:cols], w_nat[0:rows, v % 2, 0:cols], ACT.Sign,
                                         scale=COMPARE[k][0], bias=compare_bias[0:rows, k:k + 1]).then_inc(sign_set, 1)

            def turned_hi(r, v, size):
                m, ahead = UNIT[v]
                par = ahead % 2
                for h in range(HALVES):
                    act.wait_ge(w_turned, (r * 6 + v) * HALVES + h + 1)
                    dst, src = split_parts(w12T_hi, w3T_hi, m, par, h, size)
                    nc.scalar.activation(dst, src, ACT.Copy).then_inc(w_hi_done, 1)

            def silu(r, p, sb_, rows):
                tile, par = r * 2 + p, sb_ % 2
                act.wait_ge(gate_done, tile * SB + sb_ + 1)
                act.wait_ge(h_lo_done[par], tile * 2 + sb_ // 2 + 1)
                nc.scalar.activation(hidden[0:rows, par], bank[0:rows, GATE + par], ACT.Silu,
                                     scale=un_scale[0:rows, 0:1]).then_inc(silu_done, 1)

            def hidden_hi(r, p, sb_, rows):
                tile, par = r * 2 + p, sb_ % 2
                act.wait_ge(hidden_done[par], tile * 2 + sb_ // 2 + 2)
                nc.scalar.activation(hT_hi[0:rows, p, sb_ * BANK:(sb_ + 1) * BANK], hidden[0:rows, par], ACT.Copy).then_inc(h_hi_done, 1)

            def drain(r, st):
                act.wait_ge(down_done[1], r * T + st + 1)
                act.wait_ge(summed, r * T + st + 1)
                nc.scalar.activation(down_part[:, st % 2], down_bank(st, 1), ACT.Copy,
                                     scale=un_scale[:, 2:3]).then_inc(down_read[1], 1)

            def body(r, sizes):
                for w in range(WINDOWS):
                    v = AHEAD + w
                    steps, turn = steps_of(w, sizes), size_of(v - 1, sizes)
                    if w < 4:
                        compare(r, portion(steps, 0, 4), sizes)
                        if w > 0:
                            hidden_hi(r, (w - 1) // 2, (w - 1) % 2 * 2 + 1, sizes[(w - 1) // 2])
                        compare(r, portion(steps, 1, 4), sizes)
                        silu(r, w // 2, w % 2 * 2, sizes[w // 2])
                        if turn:
                            turned_hi(r, v - 1, turn)
                        compare(r, portion(steps, 2, 4), sizes)
                        hidden_hi(r, w // 2, w % 2 * 2, sizes[w // 2])
                        compare(r, portion(steps, 3, 4), sizes)
                        silu(r, w // 2, w % 2 * 2 + 1, sizes[w // 2])
                        continue
                    tiles = T // 2
                    for i in range(tiles):
                        compare(r, portion(steps, i, tiles), sizes)
                        if w == 4 and i == 1:
                            hidden_hi(r, 1, SB - 1, sizes[1])
                        drain(r, (w - 4) * tiles + i)
                        if i == tiles // 2 - 1 and turn:
                            turned_hi(r, v - 1, turn)

            act.dma_start(acc[:], x1_dram.rearrange("(t p) e -> p t e", p=P)).then_inc(acc_in, 16)
            compare(0, first_units[0], FULL)
            compare(0, first_units[1], FULL)
            turned_hi(0, 0, P)
            turned_hi(0, 1, P)
            compare(0, first_units[2], FULL)
            rounds(act, body)

        @block.vector
        def _(dve):
            V = nc.vector

            def sum_steps(r, steps, sizes):
                for v, k in steps:
                    rows, cols = rows_of(UNIT[v][0], size_of(v, sizes))
                    unit = r * 6 + v
                    total = codes[0:rows, v % 2, 0:cols]
                    dve.wait_ge(sign_set, unit * LEVELS + k + 1)
                    part = signs[0:rows, ring(v, k), 0:cols]
                    if k == 0 and v >= 2:
                        dve.wait_ge(w_turned, (unit - 1) * HALVES)
                    for h, (done, credit) in enumerate(((left_sum, 0), (sign_used, SIGN_RING))):
                        half = slice(h * cols // 2, (h + 1) * cols // 2)
                        if k == 0:
                            V.tensor_scalar(total[:, half], part[:, half], HALF_STEP[0], None, ALU.mult).then_inc(done, 1)
                        else:
                            dve.wait_ge(done, unit * LEVELS + credit + k)
                            V.scalar_tensor_tensor(total[:, half], part[:, half], HALF_STEP[k], total[:, half],
                                                   ALU.mult, ALU.add).then_inc(done, 1)

            def turned_lo(r, v, size):
                m, ahead = UNIT[v]
                par = ahead % 2
                for h in range(HALVES):
                    dve.wait_ge(w_hi_done, (r * 6 + v) * HALVES + h + 1)
                    hi, src = split_parts(w12T_hi, w3T_hi, m, par, h, size)
                    lo, _ = split_parts(w12T_lo, w3T_lo, m, par, h, size)
                    V.tensor_tensor(lo, src, hi, ALU.subtract).then_inc(w_lo_done, 1)

            def hidden_value(r, p, sb_, rows):
                tile, par = r * 2 + p, sb_ % 2
                dve.wait_ge(silu_done, tile * SB + sb_ + 1)
                dve.wait_ge(up_done, tile * SB + sb_ + 1)
                V.scalar_tensor_tensor(hidden[0:rows, par], bank[0:rows, UP + par], un_scale[0:rows, 1:2], hidden[0:rows, par],
                                       ALU.mult, ALU.mult).then_inc(hidden_done[par], 1)

            def set_scales():
                def then(ins):
                    seq.mark(ins)
                    seq.wait(dve)

                for m in range(3):
                    then(V.tensor_reduce(top[:, m:m + 1], absmax[:, :, m], AX.XY, ALU.max))
                then(V.tensor_tensor(squares, absmax[:, :, 0:2], absmax[:, :, 0:2], ALU.mult))
                then(V.tensor_reduce(norms, squares, AX.X, ALU.add))
                then(V.tensor_tensor(norm_prod, norms[:, :, 0], norms[:, :, 1], ALU.mult))
                V.tensor_reduce(top[:, 3:4], norm_prod, AX.X, ALU.max).then_inc(ff_max, 1)
                then(V.tensor_scalar(inv_absmax[:], absmax[:], TINY, None, ALU.max))
                V.reciprocal(inv_absmax[:], inv_absmax[:]).then_inc(inv_ready, 1)
                dve.wait_ge(ff_max_all, 1)
                V.tensor_scalar(pow2[:], top_all[:], TINY, None, ALU.max).then_inc(ff_floor, 1)
                dve.wait_ge(ff_root, 1)
                then(V.tensor_copy(pow2[:, 3:4], top_all[:, 3:4]))
                then(V.tensor_scalar(pow2[:].bitcast(I32), pow2[:].bitcast(I32), EXPONENT_BITS, None, ALU.bitwise_and))
                then(V.reciprocal(inv_pow2[:], pow2[:]))
                then(V.tensor_scalar(w_scale[:, 0:3], inv_pow2[:, 0:3], 2.0 ** 14, None, ALU.mult))
                for m in range(3):
                    last = V.tensor_scalar(absmax[:, :, m], absmax[:, :, m], w_scale[:, m:m + 1], None, ALU.mult)
                last.then_inc(scaled, 1)
                then(V.tensor_scalar(un_scale[:, 0:2], pow2[:, 0:2], 2.0 ** -14 / X_SCALE, None, ALU.mult))
                then(V.tensor_scalar(un_scale[:, 1:2], un_scale[:, 1:2], inv_pow2[:, 3:4], 2.0 ** -2, ALU.mult, ALU.mult))
                then(V.tensor_scalar(un_scale[:, 2:3], pow2[:, 2:3], pow2[:, 3:4], 2.0 ** (2 - 14), ALU.mult, ALU.mult))

            def add_down(r, st):
                dve.wait_ge(acc_in, 16)
                dve.wait_ge(down_done[0], r * T + st + 1)
                V.scalar_tensor_tensor(acc[:, st, 0:BANK], down_bank(st, 0), un_scale[:, 2:3], acc[:, st, 0:BANK],
                                       ALU.mult, ALU.add).then_inc(down_read[0], 1)

            def body(r, sizes):
                for w in range(WINDOWS):
                    v = AHEAD + w
                    steps, turn = steps_of(w, sizes), size_of(v - 1, sizes)
                    if w < 4:
                        sum_steps(r, portion(steps, 0, 2), sizes)
                        hidden_value(r, w // 2, w % 2 * 2, sizes[w // 2])
                        if turn:
                            turned_lo(r, v - 1, turn)
                        sum_steps(r, portion(steps, 1, 2), sizes)
                        hidden_value(r, w // 2, w % 2 * 2 + 1, sizes[w // 2])
                        continue
                    tiles = T // 2
                    for i in range(tiles):
                        add_down(r, (w - 4) * tiles + i)
                        sum_steps(r, portion(steps, i, tiles), sizes)
                        if i == tiles // 2 - 1 and turn:
                            turned_lo(r, v - 1, turn)

            set_scales()
            for i in range(2):
                dve.sem_inc(hidden_done[i], 1)
                dve.sem_inc(h_lo_done[i], 1)
                dve.sem_inc(down_read[i], 2)
            dve.sem_inc(sign_used, SIGN_RING)
            sum_steps(0, first_units[0], FULL)
            sum_steps(0, first_units[1], FULL)
            turned_lo(0, 0, P)
            turned_lo(0, 1, P)
            sum_steps(0, first_units[2], FULL)
            rounds(dve, body)

        @block.tensor
        def _(pe):
            def turn(r, v, size):
                m, _ = UNIT[v]
                unit, slot = r * 6 + v, v % 2
                pe.wait_ge(rounded, unit + 1)
                pe.wait_ge(w_lo_done, unit * HALVES)
                for h in range(HALVES):
                    for c in range(4 * h, 4 * h + 4):
                        if m < 2:
                            last = nc.tensor.transpose(bank[:, TURN + h, c % 4 * P:c % 4 * P + size],
                                                       codes[0:size, slot, c * P:(c + 1) * P], ident[0:size, 0:size])
                        else:
                            last = nc.tensor.transpose(bank[0:size, TURN + h, c % 4 * P:(c % 4 + 1) * P],
                                                       codes[:, slot, c * size:(c + 1) * size], ident[:])
                    last.then_inc(w_turned, 1)

            def gate_up(r, p, sb_, rows):
                tile, par = r * 2 + p, sb_ % 2
                toks = slice(sb_ * ST_BLOCK, (sb_ + 1) * ST_BLOCK)
                pe.wait_ge(x2_in[sb_], 32)
                pe.wait_ge(hidden_done[par], tile * 2 + sb_ // 2 + 1)
                if p == 0 and sb_ == 0:
                    for h in range(HALVES):
                        pe.wait_ge(down_read[h], r * T + 1)
                for m, to, done in ((0, GATE, gate_done), (1, UP, up_done)):
                    if sb_ == 0:
                        pe.wait_ge(w_lo_done, (r * 6 + 2 * p + m + 1) * HALVES)
                    dst = bank[0:rows, to + par]
                    for c in range(C):
                        hi, lo = w12T_hi[:, p, m, c, 0:rows], w12T_lo[:, p, m, c, 0:rows]
                        nc.tensor.matmul(dst, hi, x2T_hi[:, toks, c], start=c == 0, stop=False)
                        nc.tensor.matmul(dst, hi, x2T_lo[:, toks, c], start=False, stop=False)
                        last = nc.tensor.matmul(dst, lo, x2T_hi[:, toks, c], start=False, stop=c == C - 1)
                    last.then_inc(done, 1)

            def down(r, st, rows):
                toks = slice(st * P, (st + 1) * P)
                if st % ST_BLOCK == 0:
                    sb_ = st // ST_BLOCK
                    pe.wait_ge(h_lo_done[sb_ % 2], (r * 2 + 1) * 2 + sb_ // 2 + 2)
                if st == 0:
                    pe.wait_ge(hidden_done[0], (r * 2 + 1) * 2 + 3)
                for h in range(HALVES):
                    cols = slice(h * BANK, (h + 1) * BANK)
                    pe.wait_ge(down_read[h], r * T + st + 1)
                    for p in range(GROUP):
                        k = slice(0, rows[p])
                        dst = down_bank(st, h)
                        nc.tensor.matmul(dst, hT_hi[k, p, toks], w3T_hi[k, p, cols], start=p == 0, stop=False)
                        nc.tensor.matmul(dst, hT_hi[k, p, toks], w3T_lo[k, p, cols], start=False, stop=False)
                        last = nc.tensor.matmul(dst, hT_lo[k, p, toks], w3T_hi[k, p, cols], start=False, stop=p == GROUP - 1)
                    last.then_inc(down_done[h], 1)

            def body(r, sizes):
                for w in range(WINDOWS):
                    v = AHEAD - 1 + w
                    size = size_of(v, sizes)
                    if w < 4:
                        gate_up(r, w // 2, w % 2 * 2, sizes[w // 2])
                        if size:
                            turn(r, v, size)
                        gate_up(r, w // 2, w % 2 * 2 + 1, sizes[w // 2])
                        continue
                    if w == 4:
                        pe.wait_ge(w_lo_done, (r * 6 + 6) * HALVES)
                    for i in range(T // 2):
                        down(r, (w - 4) * (T // 2) + i, sizes[0:GROUP])
                        if i == T // 4 - 1 and size:
                            turn(r, v, size)

            turn(0, 0, P)
            turn(0, 1, P)
            rounds(pe, body)


_INS = ["L0_attn_hidden_states", "L0_attn_wq", "L0_attn_bq", "L0_attn_wk", "L0_attn_bk", "L0_attn_wv", "L0_attn_bv",
        "L0_ffn_w1", "L0_ffn_w2", "L0_ffn_w3"]


def kernel(**inputs):
    import concourse.bacc as bacc
    from concourse.bass_utils import run_bass_kernel_spmd

    nc = bacc.Bacc("TRN2", target_bir_lowering=False, num_devices=1)
    arrays, args = {}, []
    for name in _INS:
        a = np.ascontiguousarray(inputs[name])
        arrays[f"in_{name}"] = a
        args.append(nc.dram_tensor(f"in_{name}", a.shape, mybir.dt.from_np(a.dtype), kind="ExternalInput").ap())
    shape = arrays["in_L0_attn_hidden_states"].shape
    out = nc.dram_tensor("out", shape, F32, kind="ExternalOutput").ap()
    layer(nc, *args, out)
    r = run_bass_kernel_spmd(nc, [arrays], core_ids=[0])
    return r.results[0]["out"]
```

```python
from contextlib import ExitStack

import numpy as np

import concourse.bass as bass
from concourse import mybir

F32 = mybir.dt.float32
F16 = mybir.dt.float16
I32 = mybir.dt.int32
I8 = mybir.dt.int8
ALU = mybir.AluOpType
ACT = mybir.ActivationFunctionType
AX = mybir.AxisListType
ALL_MAX = bass.bass_isa.ReduceOp.max

P = 128
QUAD = 32
BANK = 512
EPS = 1e-5
X_SCALE = 2.0 ** 10
TINY = 2.0 ** -60
EXPONENT_BITS = 0x7F800000
BLOCK = 64

NF4 = np.array([-1.0, -0.6961928009986877, -0.5250730514526367, -0.39491748809814453,
                -0.28444138169288635, -0.18477343022823334, -0.09105003625154495, 0.0,
                0.07958029955625534, 0.16093020141124725, 0.24611230194568634,
                0.33791524171829224, 0.44070982933044434, 0.5626170039176941,
                0.7229568362236023, 1.0], dtype=np.float32)
LEVELS = len(NF4) - 1
BOUNDS = (NF4[:-1] + NF4[1:]) * np.float32(0.5)


def strict_compare(bound):
    b = np.float64(bound)
    middle = (b + np.float64(np.nextafter(bound, np.float32(2.0)))) / 2
    best = None
    for k in range(2000):
        scale = np.float32(1.0 + k * 2.0 ** -23)
        bias = np.float32(np.float64(scale) * middle)
        off = abs(np.float64(bias) / np.float64(scale) - middle)
        if best is None or off < best[0]:
            best = (off, float(scale), -float(bias))
    return best[1], best[2]


COMPARE = [strict_compare(b) for b in BOUNDS]
GRID = 2.0 ** 25
HALF_STEP = [float(np.round((np.float64(NF4[i + 1]) - np.float64(NF4[i])) / 2 * GRID) / GRID)
             for i in range(LEVELS)]
SIGN_RING = 5



class Count:

    def __init__(self, sem):
        self.sem, self.base, self.off = sem, 0, 0

    def at(self, base):
        self.base, self.off = base, 0

    def mark(self, ins):
        self.off += 1
        return ins.then_inc(self.sem, 1)

    def wait(self, eng):
        eng.wait_ge(self.sem, self.base + self.off)


def layer(nc, x, wq, bq, wk, bk, wv, bv, w1, w2, w3, out):
    TOK, E = x.shape[-2:]
    FF = w1.shape[0]
    HD = QUAD
    HEADS = E // HD
    C = E // P
    T = TOK // P
    SB = TOK // BANK
    ST_BLOCK = BANK // P
    FT = FF // P
    REST = FF - FT * P
    NB = E // BLOCK
    HALVES = E // BANK
    GROUP = 2
    x_dram = x.rearrange("a s e -> (a s) e")
    x1_dram = nc.dram_tensor("x1", [TOK, E], F32).ap()
    x2_hi_dram = nc.dram_tensor("x2_hi_dram", [TOK, E], F16).ap()
    x2_lo_dram = nc.dram_tensor("x2_lo_dram", [TOK, E], F16).ap()

    with ExitStack() as whole:
        def sem(name):
            return whole.enter_context(nc.semaphore(name))

        def keep(name, shape, dt=F32):
            return whole.enter_context(nc.sbuf_tensor(name, shape, dt))

        bank = whole.enter_context(nc.psum_tensor("bank", [P, 8, BANK], F32))

        ident = keep("ident", [P, P])
        compare_bias = keep("compare_bias", [P, LEVELS])
        power = keep("power", [P, 2])
        absmax = keep("absmax", [P, FT + 1, 3, NB])
        top = keep("top", [P, 4])
        top_all = keep("top_all", [P, 4])
        pow2 = keep("pow2", [P, 4])
        inv_pow2 = keep("inv_pow2", [P, 4])
        w_scale = keep("w_scale", [P, 4])
        un_scale = keep("un_scale", [P, 4])
        stats = keep("stats", [P, 2, 6])
        mean_var = keep("mean_var", [P, 2])
        var_eps = keep("var_eps", [P, 1])
        rstd = keep("rstd", [P, 1])
        row_max = keep("row_max", [P, QUAD])
        row_sum = keep("row_sum", [P, QUAD])
        inv_sum = keep("inv_sum", [P, QUAD])

        consts_set = sem("consts_set")
        dve_seq = sem("dve_seq")

        attend_sync, attend_gpsimd, attend_vector, attend_scalar, attend_tensor, ff_raw, x1_out, x2_out = attention(nc, locals())
        feed_sync, feed_gpsimd, feed_vector, feed_scalar, feed_tensor = feed_forward(nc, locals())

        def both(attend_program, feed_program, eng):
            feed = feed_program(eng)
            attend_program(eng, feed)
            for _ in feed:
                pass

        with nc.Block() as block:

            @block.sync
            def _(sp):
                both(attend_sync, feed_sync, sp)

            @block.gpsimd
            def _(pool):
                both(attend_gpsimd, feed_gpsimd, pool)

            @block.vector
            def _(dve):
                both(attend_vector, feed_vector, dve)

            @block.scalar
            def _(act):
                both(attend_scalar, feed_scalar, act)

            @block.tensor
            def _(pe):
                both(attend_tensor, feed_tensor, pe)


def attention(nc, g):
    C, T, E, NB, FT, REST, HEADS, HD, ST_BLOCK = (g[k] for k in "C T E NB FT REST HEADS HD ST_BLOCK".split())
    bank, ident, sem = g["bank"], g["ident"], g["sem"]
    top, top_all, pow2, inv_pow2, w_scale, un_scale = (g[k] for k in "top top_all pow2 inv_pow2 w_scale un_scale".split())
    stats, mean_var, var_eps, rstd = (g[k] for k in "stats mean_var var_eps rstd".split())
    row_max, row_sum, inv_sum, absmax = (g[k] for k in "row_max row_sum inv_sum absmax".split())
    power, compare_bias, consts_set, dve_seq = (g[k] for k in "power compare_bias consts_set dve_seq".split())
    x_dram, x1_dram, x2_hi_dram, x2_lo_dram = (g[k] for k in "x_dram x1_dram x2_hi_dram x2_lo_dram".split())
    w_qkv = [g["wq"], g["wk"], g["wv"]]
    b_qkv = [g["bq"], g["bk"], g["bv"]]
    w1, w2, w3 = g["w1"], g["w2"], g["w3"]
    seq = Count(dve_seq)

    with ExitStack() as mine:
        def sb(name, shape, dt=F32):
            return mine.enter_context(nc.sbuf_tensor(name, shape, dt))

        wT_hi = sb("wT_hi", [P, 3, C, E], F16)
        wT_lo = sb("wT_lo", [P, 3, C, E], F16)

        lo_sums = sb("lo_sums", [P, 3 * C])
        lo_sum = sb("lo_sum", [P, 2])

        LOADS = 8
        with nc.sbuf_tensor("w_raw0", [P, C, E], F32) as w_raw0:
            pass
        bias = sb("bias", [P, 3, E])
        x_nat = sb("x_nat", [P, 2, E])
        xT_hi = sb("xT_hi", [P, 2, C, P], F16)
        xT_lo = sb("xT_lo", [P, 2, C, P], F16)
        qT = sb("qT", [P, QUAD, HEADS])
        TURN = 6

        w_in = [[sem(f"w_in{m}_{k}") for k in range(LOADS)] for m in range(3)]
        w_seen = sem("w_seen")
        lo_looked = sem("lo_looked")
        lo_sum_ready = sem("lo_sum_ready")
        lo_known = sem("lo_known")
        local_max = sem("local_max")
        global_max = sem("global_max")
        scale_set = sem("scale_set")
        w_turned = sem("w_turned")
        w_hi_done = sem("w_hi_done")
        w_lo_done = sem("w_lo_done")
        bias_in = sem("bias_in")
        x_in = [sem("x_in0"), sem("x_in1")]
        res_in = sem("res_in")
        var_ready = sem("var_ready")
        rstd_ready = sem("rstd_ready")
        normed = sem("normed")
        x_turned = sem("x_turned")
        x_hi_done = sem("x_hi_done")
        x_lo_done = sem("x_lo_done")
        held = sem("held")

        def load_x(sp, n, slot):
            sp.dma_start(x_nat[:, slot], x_dram[bass.ds(n * P, P), :]).then_inc(x_in[slot], 16)

        def load_res(sp, n):
            sp.dma_start(x_res[:], x_dram[bass.ds(n * P, P), :]).then_inc(res_in, 16)

        def moments(dve, rows, part, mv, ve, ready):
            for h in range(2):
                last = nc.vector.bn_stats(part[:, h], rows[:, h * BANK:(h + 1) * BANK])
            seq.mark(last)
            seq.wait(dve)
            dve.sem_inc(held, 1)
            seq.mark(nc.vector.bn_aggr(mv[:], part[:].rearrange("p h s -> p (h s)")))
            seq.wait(dve)
            nc.vector.tensor_scalar(ve[:], mv[:, 1:2], EPS, None, ALU.add).then_inc(ready, 1)

        def norm_stats(dve, n, slot, loaded):
            dve.wait_ge(x_in[slot], 16 * loaded)
            moments(dve, x_nat[:, slot], stats, mean_var, var_eps, var_ready)

        def inv_std(pool, n):
            pool.wait_ge(var_ready, n + 1)
            nc.gpsimd.tensor_tensor(rstd[:], var_eps[:], power[:, 0:1], ALU.pow).then_inc(rstd_ready, 1)

        def norm_apply(dve, n, slot):
            dve.wait_ge(rstd_ready, n + 1)
            nc.vector.tensor_scalar(x_nat[:, slot], x_nat[:, slot], mean_var[:, 0:1], rstd[:, 0:1],
                                    ALU.subtract, ALU.mult).then_inc(normed, 1)

        def turn(rows, done):
            for h in range(2):
                for c in range(4 * h, 4 * h + 4):
                    last = nc.tensor.transpose(bank[:, TURN + h, (c % 4) * P:(c % 4 + 1) * P], rows[:, c * P:(c + 1) * P], ident[:])
                last.then_inc(done, 1)

        def split_hi(act, n, hi, turned, hi_done):
            for h in range(2):
                act.wait_ge(turned, 2 * n + h + 1)
                nc.scalar.activation(hi[:, 4 * h:4 * h + 4].rearrange("p c s -> p (c s)"), bank[:, TURN + h],
                                     ACT.Copy, scale=X_SCALE).then_inc(hi_done, 1)

        def split_lo(dve, n, lo, hi, hi_done, lo_done):
            for h in range(2):
                dve.wait_ge(hi_done, 2 * n + h + 1)
                nc.vector.scalar_tensor_tensor(lo[:, 4 * h:4 * h + 4].rearrange("p c s -> p (c s)"), bank[:, TURN + h], X_SCALE,
                                               hi[:, 4 * h:4 * h + 4].rearrange("p c s -> p (c s)"),
                                               ALU.mult, ALU.subtract).then_inc(lo_done, 1)

        RING = 4
        FILLS = C * 2
        PART = C // LOADS
        LOOKS = {4 + k: k for k in range(LOADS)}
        SCALE = 13
        STATS, NORM = 4, 8
        with (nc.sbuf_tensor("w_raw1", [P, C, E], F32) as w_raw1, nc.sbuf_tensor("w_raw2", [P, C, E], F32) as w_raw2,
              nc.sbuf_tensor("part_max", [P, 3, LOADS], F32) as part_max,
              nc.sbuf_tensor("lo_abs", [P, E], F16) as lo_abs, nc.Block() as block):
            w_raw = [w_raw0, w_raw1, w_raw2]

            @block.sync
            def _(sp):
                for m in range(3):
                    rows = w_qkv[m].rearrange("(t p) d -> p t d", p=P)
                    for k in range(LOADS):
                        part = slice(k * PART, (k + 1) * PART)
                        sp.dma_start(w_raw[m][:, part], rows[:, part]).then_inc(w_in[m][k], 16)
                sp.wait_ge(w_turned, FILLS)
                load_x(sp, 0, 0)
                load_x(sp, 1, 1)
                for m in range(3):
                    sp.dma_start(bias[:, m], b_qkv[m].rearrange("(o n) -> o n", o=1).to_broadcast([P, E])).then_inc(bias_in, 16)

            @block.gpsimd
            def _(pool):
                pool.memset(ident[:], 0.0).then_inc(consts_set, 1)
                pool.memset(absmax[:], 0.0).then_inc(consts_set, 1)
                pool.memset(power[:, 0:1], -0.5).then_inc(consts_set, 1)
                pool.memset(power[:, 1:2], 0.5).then_inc(consts_set, 1)
                for i in range(LEVELS):
                    pool.memset(compare_bias[:, i:i + 1], COMPARE[i][1]).then_inc(consts_set, 1)
                pool.wait_ge(consts_set, 1)
                pool.affine_select(out=ident[:], in_=ident[:], compare_op=ALU.not_equal, fill=1.0, base=0,
                                   pattern=[[-1, P]], channel_multiplier=1).then_inc(consts_set, 1)
                for m in range(3):
                    pool.wait_ge(local_max, m + 1)
                    nc.gpsimd.partition_all_reduce(top_all[:, m:m + 1], top[:, m:m + 1], P, ALL_MAX).then_inc(global_max, 1)
                inv_std(pool, 0)
                pool.wait_ge(lo_sum_ready, 1)
                nc.gpsimd.partition_all_reduce(lo_sum[:, 1:2], lo_sum[:, 0:1], P, ALL_MAX).then_inc(lo_known, 1)

            @block.vector
            def _(dve):
                def look(m, k):
                    dve.wait_ge(w_in[m][k], 16)
                    nc.vector.tensor_reduce(part_max[:, m, k:k + 1], w_raw[m][:, k * PART:(k + 1) * PART].rearrange("p t d -> p (t d)"),
                                            AX.X, ALU.max, apply_absolute_value=True).then_inc(w_seen, 1)
                    if k == LOADS - 1:
                        dve.wait_ge(w_seen, LOADS * (m + 1))
                        nc.vector.tensor_reduce(top[:, m:m + 1], part_max[:, m], AX.X, ALU.max).then_inc(local_max, 1)

                def find_scale(m):
                    col = slice(m, m + 1)
                    dve.wait_ge(global_max, m + 1)
                    seq.mark(nc.vector.tensor_scalar(pow2[:, col], top_all[:, col], TINY, None, ALU.max))
                    seq.wait(dve)
                    seq.mark(nc.vector.tensor_scalar(pow2[:, col].bitcast(I32), pow2[:, col].bitcast(I32),
                                                     EXPONENT_BITS, None, ALU.bitwise_and))
                    seq.wait(dve)
                    seq.mark(nc.vector.reciprocal(inv_pow2[:, col], pow2[:, col]))
                    seq.mark(nc.vector.tensor_scalar(un_scale[:, col], pow2[:, col], 2.0 ** -14 / X_SCALE, None, ALU.mult))
                    seq.wait(dve)
                    nc.vector.tensor_scalar(w_scale[:, col], inv_pow2[:, col], 2.0 ** 14, None, ALU.mult).then_inc(scale_set, 1)

                for k in range(LOADS):
                    look(0, k)
                find_scale(0)
                for m in range(3):
                    dve.wait_ge(scale_set, m + 1)
                    for f in range(FILLS):
                        n = m * FILLS + f
                        c, half = f // 2, f % 2
                        dst = (slice(None), m, c, slice(half * BANK, half * BANK + BANK))
                        dve.wait_ge(w_hi_done, n + 1)
                        nc.vector.scalar_tensor_tensor(wT_lo[dst], bank[:, n % RING], w_scale[:, m:m + 1], wT_hi[dst],
                                                       ALU.mult, ALU.subtract).then_inc(w_lo_done, 1)
                        if m < 2 and f in LOOKS:
                            look(m + 1, LOOKS[f])
                        elif m < 2 and f == SCALE:
                            find_scale(m + 1)
                        elif m == 2 and f == STATS:
                            norm_stats(dve, 0, 0, 1)
                        elif m == 2 and f == NORM:
                            norm_apply(dve, 0, 0)
                split_lo(dve, 0, xT_lo[:, 0], xT_hi[:, 0], x_hi_done, x_lo_done)
                dve.wait_ge(lo_looked, 3 * C)
                nc.vector.tensor_reduce(lo_sum[:, 0:1], lo_sums[:], AX.X, ALU.max).then_inc(lo_sum_ready, 1)

            @block.scalar
            def _(act):
                def look_at_lo(q):
                    act.wait_ge(w_lo_done, 2 * q + 2)
                    if q > 0:
                        act.wait_ge(lo_looked, q)
                    nc.scalar.activation(lo_abs[:], wT_lo[:, q // C, q % C], ACT.Abs,
                                         accum_out=lo_sums[:, q:q + 1]).then_inc(lo_looked, 1)

                for m in range(3):
                    act.wait_ge(scale_set, m + 1)
                    for f in range(FILLS):
                        n = m * FILLS + f
                        c, half = f // 2, f % 2
                        act.wait_ge(w_turned, n + 1)
                        nc.scalar.activation(wT_hi[:, m, c, half * BANK:half * BANK + BANK], bank[:, n % RING],
                                             ACT.Copy, scale=w_scale[:, m:m + 1]).then_inc(w_hi_done, 1)
                        if half == 1 and n > 1:
                            look_at_lo(n // 2 - 1)
                split_hi(act, 0, xT_hi[:, 0], x_turned, x_hi_done)
                look_at_lo(3 * C - 1)

            @block.tensor
            def _(pe):
                pe.wait_ge(consts_set, 5 + LEVELS)
                for m in range(3):
                    for k in range(LOADS):
                        pe.wait_ge(w_in[m][k], 16)
                    for f in range(FILLS):
                        n = m * FILLS + f
                        c, half = f // 2, f % 2
                        if n >= RING:
                            pe.wait_ge(w_lo_done, n - RING + 1)
                        for j in range(BANK // P):
                            t = half * (BANK // P) + j
                            last = nc.tensor.transpose(bank[:, n % RING, j * P:(j + 1) * P],
                                                       w_raw[m][:, t, c * P:(c + 1) * P], ident[:])
                        last.then_inc(w_turned, 1)
                pe.wait_ge(normed, 1)
                turn(x_nat[:, 0], x_turned)

        qkv = sb("qkv", [P, 3, E])
        x_res = sb("x_res", [P, E])
        x2_hi = sb("x2_hi", [P, C, P], F16)
        x2_lo = sb("x2_lo", [P, C, P], F16)
        kT = sb("kT", [P, QUAD, HEADS])
        vT = sb("vT", [P, QUAD, HD])
        q_diag = sb("q_diag", [P, QUAD, P])
        p_diag = sb("p_diag", [P, QUAD, P])
        probs = sb("probs", [P, QUAD, HEADS])
        flipped = sb("flipped", [P, E])
        ff_raw = sb("ff_raw", [P, E])
        stats2 = sb("stats2", [P, 2, 6])
        mean_var2 = sb("mean_var2", [P, 2])
        var_eps2 = sb("var_eps2", [P, 1])
        rstd2 = sb("rstd2", [P, 1])

        diag_zero = sem("diag_zero")
        projected = sem("projected")
        evacuated = sem("evacuated")
        q_ready = sem("q_ready")
        q_placed = sem("q_placed")
        k_ready = sem("k_ready")
        v_ready = sem("v_ready")
        scores_done = sem("scores_done")
        centered = sem("centered")
        exp_done = sem("exp_done")
        p_ready = sem("p_ready")
        p_placed = sem("p_placed")
        context_done = sem("context_done")
        ctx_read = sem("ctx_read")
        ctx_ready = sem("ctx_ready")
        res_done = sem("res_done")
        x1_out = sem("x1_out")
        var2_ready = sem("var2_ready")
        rstd2_ready = sem("rstd2_ready")
        normed2 = sem("normed2")
        x2_turned = sem("x2_turned")
        x2_hi_done = sem("x2_hi_done")
        x2_lo_done = sem("x2_lo_done")
        x2_out = sem("x2_out")
        ff_in = sem("ff_in")
        absmax_done = sem("absmax_done")

        PROJ_RING = 4
        mixing = bank[:, 4:6].rearrange("p b n -> p (b n)")
        scores = mixing.rearrange("p (t h) -> p t h", h=HEADS)
        context = mixing.rearrange("p (t d) -> p t d", d=HD)
        quadrants = [slice(a * QUAD, (a + 1) * QUAD) for a in range(P // QUAD)]

        LOOP = (T - 4) // 2
        MARKS = 7

        def all_steps(eng, step, feed):
            first_steps(step)
            middle_steps(eng, step, feed)
            last_steps(step, feed)

        def first_steps(step):
            step(0, 0, None, attend=False, end=False)
            step(1, 1, None, end=False)

        def middle_steps(eng, step, feed):
            with eng.Fori(0, LOOP) as it:
                for u in range(2):
                    step(it * 2 + 2 + u, u, it)
            step(T - 2, 0, None)
            step(T - 1, 1, None, normalize=False, feed=feed)

        def last_steps(step, feed):
            step(T, 0, None, project=False, normalize=False, feed=feed)
            step(T + 1, 1, None, project=False, normalize=False, attend=False, feed=feed)

        IN_LOOP = (5, 4)
        assert FT == 2 + 3 * LOOP + 1 and REST

        def looks(n, u, it):
            if it is not None:
                places = [u * IN_LOOP[0] + k for k in range(IN_LOOP[u])]
                return [(it * 3 + 2 + q // 3, q % 3, it * 9 + 6 + q, P) for q in places]
            tiles = {0: (0,), 1: (1,), T - 2: (FT - 1, FT)}.get(n, ())
            return [(tile, m, tile * 3 + m, P if tile < FT else REST) for tile in tiles for m in range(3)]

        def sync(sp, feed):
            def load_ff(tile, m, j, rows):
                first = tile * P
                sp.wait_ge(absmax_done, j + 1)
                if m == 2:
                    sp.sem_inc(held, 1)
                if m < 2:
                    sp.dma_start(ff_raw[0:rows], (w1, w2)[m][bass.ds(first, rows), :]).then_inc(ff_in, 16)
                else:
                    sp.dma_start(ff_raw[:, 0:C * rows].rearrange("p (t h) -> p t h", t=C),
                                 w3.rearrange("(t p) h -> p t h", p=P)[:, :, bass.ds(first, rows)]).then_inc(ff_in, 16)

            def step(n, u, it, project=True, normalize=True, attend=True, end=True, feed=None):
                todo = looks(n, u, it)
                if normalize and not (it is None and n + 2 >= T):
                    sp.wait_ge(x_turned, 2 * n + 2)
                    load_x(sp, n + 2, u)
                for look in todo[:1]:
                    load_ff(*look)
                if end:
                    sp.wait_ge(res_done, n - 1)
                    sp.dma_start(x1_dram[bass.ds((n - 2) * P, P), :], x_res[:]).then_inc(x1_out, 16)
                if feed and attend and not project:
                    sp.wait_ge(projected, 6 * n)
                    sp.wait_ge(evacuated, 6 * n)
                    sp.wait_ge(q_placed, n)
                    sp.wait_ge(v_ready, n)
                    sp.wait_ge(x2_out, 32 * (T - ST_BLOCK + 1))
                    next(feed)
                if feed and not attend:
                    next(feed)
                if feed and project:
                    sp.wait_ge(projected, 6 * n + 2)
                    next(feed)
                for look in todo[1:4]:
                    load_ff(*look)
                if end and attend:
                    sp.wait_ge(x2_turned, 2 * (n - 1))
                    load_res(sp, n - 1)
                for look in todo[4:]:
                    load_ff(*look)
                if end:
                    sp.wait_ge(x2_lo_done, 2 * n)
                    sp.sem_inc(held, 1)
                    for dram, part in ((x2_hi_dram, x2_hi), (x2_lo_dram, x2_lo)):
                        sp.dma_start(dram[bass.ds((n - 2) * P, P), :], part[:].rearrange("p c s -> p (c s)")).then_inc(x2_out, 16)
                if feed and attend and not project:
                    next(feed)

            load_res(sp, 0)
            sp.sem_inc(x2_out, 32)
            all_steps(sp, step, feed)
            sp.wait_ge(x1_out, 16 * T)
            sp.wait_ge(x2_out, 32 * (T + 1))

        def gpsimd(pool, feed):
            def step(n, u, it, project=True, normalize=True, attend=True, end=True, feed=None):
                if normalize:
                    inv_std(pool, n + 1)
                if end:
                    pool.wait_ge(ctx_ready, n - 1)
                    pool.wait_ge(res_in, 16 * (n - 1))
                    nc.gpsimd.tensor_tensor(x_res[:], x_res[:], flipped[:], ALU.add).then_inc(res_done, 1)
                    pool.wait_ge(var2_ready, n - 1)
                    nc.gpsimd.tensor_tensor(rstd2[:], var_eps2[:], power[:, 0:1], ALU.pow).then_inc(rstd2_ready, 1)
                if feed and attend:
                    next(feed)

            pool.memset(q_diag[:], 0.0).then_inc(diag_zero, 1)
            pool.memset(p_diag[:], 0.0).then_inc(diag_zero, 1)
            first_steps(step)
            middle_steps(pool, step, feed)
            last_steps(step, feed)

        def vector(dve, feed):
            def evacuate(n, u, m, h):
                i = 2 * m + h
                cols = slice(h * BANK, (h + 1) * BANK)
                dve.wait_ge(projected, 6 * n + i + 1)
                nc.vector.scalar_tensor_tensor(qkv[:, m, cols], bank[:, (6 * u + i) % PROJ_RING], un_scale[:, m:m + 1],
                                               bias[:, m, cols], ALU.mult, ALU.add).then_inc(evacuated, 1)

            def look_at(tile, m, j, rows):
                dve.wait_ge(ff_in, 16 * (j + 1))
                if m < 2:
                    part, blocks = slice(0, rows), NB
                else:
                    part, blocks = slice(0, P), C * rows // BLOCK
                if rows == P:
                    to = absmax[:].rearrange("p t m b -> p (t m b)")[:, bass.ds(j * NB, NB)]
                else:
                    to = absmax[part, tile, m, 0:NB] if m < 2 else absmax[:, tile, m, 0::P // rows]
                nc.vector.tensor_reduce(to, ff_raw[part, 0:blocks * BLOCK].rearrange("p (b e) -> p b e", e=BLOCK),
                                        AX.X, ALU.max, apply_absolute_value=True).then_inc(absmax_done, 1)

            def step(n, u, it, project=True, normalize=True, attend=True, end=True, feed=None):
                todo = looks(n, u, it)

                def look():
                    if todo:
                        look_at(*todo.pop(0))

                if it is not None:
                    seq.at(before_loop + it * (2 * MARKS) + u * MARKS)
                if end:
                    dve.wait_ge(context_done, n - 1)
                    seq.wait(dve)
                    nc.vector.tensor_tensor(probs[:], context, inv_sum[:].unsqueeze(2).to_broadcast([P, QUAD, HD]),
                                            ALU.mult).then_inc(ctx_read, 1)
                    dve.wait_ge(ctx_read, n - 1)
                    nc.vector.transpose(flipped[:].rearrange("p (h d) -> p d h", d=HD),
                                        probs[:].rearrange("p t d -> p d t")).then_inc(ctx_ready, 1)
                if attend:
                    evacuate(n - 1, 1 - u, 2, 1)
                    dve.wait_ge(evacuated, 6 * n)
                    nc.vector.transpose(vT[:].rearrange("p t d -> p d t"),
                                        qkv[:, 2].rearrange("p (h d) -> p d h", d=HD)).then_inc(v_ready, 1)
                if normalize:
                    norm_apply(dve, n + 1, 1 - u)
                look()
                if end:
                    dve.wait_ge(res_done, n - 1)
                    moments(dve, x_res[:], stats2, mean_var2, var_eps2, var2_ready)
                if feed:
                    if project:
                        dve.wait_ge(absmax_done, 3 * FT + 3 + 1)
                    next(feed)
                if project:
                    evacuate(n, u, 0, 0)
                look()
                if project:
                    evacuate(n, u, 0, 1)
                if feed and project:
                    next(feed)
                if attend:
                    dve.wait_ge(scores_done, n)
                    seq.mark(nc.vector.tensor_reduce(row_max[:], scores, AX.X, ALU.max))
                    seq.wait(dve)
                    nc.vector.tensor_tensor(probs[:], scores, row_max[:].unsqueeze(2).to_broadcast([P, QUAD, HEADS]),
                                            ALU.subtract).then_inc(centered, 1)
                    if feed:
                        next(feed)
                if end:
                    dve.wait_ge(rstd2_ready, n - 1)
                    dve.wait_ge(x1_out, 16 * (n - 1))
                    nc.vector.tensor_scalar(x_res[:], x_res[:], mean_var2[:, 0:1], rstd2[:, 0:1],
                                            ALU.subtract, ALU.mult).then_inc(normed2, 1)
                if feed and not project:
                    next(feed)
                if attend:
                    dve.wait_ge(exp_done, n)
                    if end:
                        dve.wait_ge(res_done, n - 1)
                    nc.vector.transpose(flipped[:].rearrange("p (t h) -> p t h", h=HEADS), probs[:]).then_inc(p_ready, 1)
                if normalize:
                    split_lo(dve, n + 1, xT_lo[:, 1 - u], xT_hi[:, 1 - u], x_hi_done, x_lo_done)
                if attend:
                    seq.mark(nc.vector.tensor_reduce(row_sum[:], probs[:], AX.X, ALU.add))
                    seq.wait(dve)
                    seq.mark(nc.vector.reciprocal(inv_sum[:], row_sum[:]))
                    if feed and not project:
                        next(feed)
                if project:
                    dve.wait_ge(evacuated, 6 * n + 2)
                    if not (it is None and n == 0):
                        dve.wait_ge(q_placed, n)
                    nc.vector.transpose(qT[:].rearrange("p t h -> p h t"),
                                        qkv[:, 0].rearrange("p (h d) -> p h d", d=HD)).then_inc(q_ready, 1)
                look()
                if project:
                    evacuate(n, u, 1, 0)
                look()
                if project:
                    evacuate(n, u, 1, 1)
                    dve.wait_ge(evacuated, 6 * n + 4)
                    nc.vector.transpose(kT[:].rearrange("p t h -> p h t"),
                                        qkv[:, 1].rearrange("p (h d) -> p h d", d=HD)).then_inc(k_ready, 1)
                if end:
                    split_lo(dve, n - 2, x2_lo, x2_hi, x2_hi_done, x2_lo_done)
                look()
                if project:
                    evacuate(n, u, 2, 0)
                look()
                if feed and attend:
                    next(feed)
                if it is not None or n + 2 < T:
                    norm_stats(dve, n + 2, u, n // 2 + 2 if it is None else it + 3)
                if it is not None:
                    assert seq.off == MARKS
                    if u == 1:
                        seq.at(before_loop + LOOP * 2 * MARKS)

            before_loop = 3 * 4 + 2 * 2 + 2 + 5
            dve.sem_inc(absmax_done, 1)
            dve.sem_inc(x2_lo_done, 2)
            dve.wait_ge(consts_set, 5 + LEVELS)
            seq.at(3 * 4 + 2)
            norm_stats(dve, 1, 1, 1)
            dve.wait_ge(bias_in, 48)
            all_steps(dve, step, feed)

        def scalar(act, feed):
            def place(diag, compact, done):
                for rows in quadrants:
                    last = nc.scalar.activation(diag[rows, :, rows], compact[rows].rearrange("p (t h) -> p t h", h=HEADS), ACT.Copy)
                last.then_inc(done, 1)

            def step(n, u, it, project=True, normalize=True, attend=True, end=True, feed=None):
                if feed and not project:
                    next(feed)
                if attend:
                    act.wait_ge(centered, n)
                    flat = probs[:].rearrange("p t h -> p (t h)")
                    nc.scalar.activation(flat, flat, ACT.Exp, scale=float(1 / np.sqrt(np.float32(HD)))).then_inc(exp_done, 1)
                if feed and attend and not project:
                    next(feed)
                if normalize:
                    split_hi(act, n + 1, xT_hi[:, 1 - u], x_turned, x_hi_done)
                if attend:
                    act.wait_ge(p_ready, n)
                    if end:
                        act.wait_ge(context_done, n - 1)
                    place(p_diag, flipped[:], p_placed)
                if feed and project:
                    next(feed)
                if end:
                    act.wait_ge(x2_out, 32 * (n - 1))
                    split_hi(act, n - 2, x2_hi, x2_turned, x2_hi_done)
                if project:
                    act.wait_ge(q_ready, n + 1)
                    if attend:
                        act.wait_ge(scores_done, n)
                    place(q_diag, qT[:].rearrange("p t h -> p (t h)"), q_placed)
                if feed and project:
                    next(feed)

            act.wait_ge(diag_zero, 2)
            all_steps(act, step, feed)

        def tensor(pe, feed):
            def project_one(n, u, it, m, with_lo, between=None):
                for h in range(2):
                    i = 2 * m + h
                    to = bank[:, (6 * u + i) % PROJ_RING]
                    cols = slice(h * BANK, (h + 1) * BANK)
                    if not (it is None and n == 0 and i < PROJ_RING):
                        pe.wait_ge(evacuated, 6 * n + i + 1 - PROJ_RING)
                    passes = []
                    for c in range(C):
                        passes.append((xT_hi[:, u, c], wT_hi[:, m, c, cols]))
                        if with_lo:
                            passes.append((xT_hi[:, u, c], wT_lo[:, m, c, cols]))
                        passes.append((xT_lo[:, u, c], wT_hi[:, m, c, cols]))
                    skip = len(passes) * 2 // 3 if with_lo else len(passes) // 2
                    slots = 2 * len(passes) - skip
                    for j, (x, w) in enumerate(passes):
                        ins = nc.tensor.matmul(to, x, w, start=j == 0, stop=j == len(passes) - 1)
                        if j == len(passes) - 1:
                            ins.then_inc(projected, 1)
                        slot = h * len(passes) + j - skip
                        if between and slot >= 0:
                            between(slot * QUAD // slots, (slot + 1) * QUAD // slots)

            def step(n, u, it, project=True, normalize=True, attend=True, end=True, feed=None,
                         with_lo=False):
                def score(first, last):
                    if first == 0:
                        pe.wait_ge(q_placed, n)
                        pe.wait_ge(k_ready, n)
                        if end:
                            pe.wait_ge(ctx_read, n - 1)
                    for t in range(first, last):
                        ins = nc.tensor.matmul(scores[:, t], q_diag[:, t], kT[:, t], start=True, stop=True)
                    if last == QUAD:
                        ins.then_inc(scores_done, 1)

                def mix(first, last):
                    if first == 0:
                        pe.wait_ge(p_placed, n)
                        pe.wait_ge(v_ready, n)
                    for t in range(first, last):
                        ins = nc.tensor.matmul(context[:, t], p_diag[:, t], vT[:, t], start=True, stop=True)
                    if last == QUAD:
                        ins.then_inc(context_done, 1)

                if project:
                    pe.wait_ge(x_lo_done, 2 * n + 2)
                    project_one(n, u, it, 0, with_lo, score if attend else None)
                elif attend:
                    score(0, QUAD)
                if normalize:
                    pe.wait_ge(normed, n + 2)
                    if end:
                        pe.wait_ge(x2_lo_done, 2 * (n - 1))
                    turn(x_nat[:, 1 - u], x_turned)
                if project:
                    project_one(n, u, it, 1, with_lo)
                if end:
                    pe.wait_ge(normed2, n - 1)
                    if normalize:
                        pe.wait_ge(x_lo_done, 2 * (n + 2))
                    else:
                        pe.wait_ge(x2_lo_done, 2 * (n - 1))
                    turn(x_res[:], x2_turned)
                if project:
                    project_one(n, u, it, 2, with_lo, mix if attend else None)
                elif attend:
                    mix(0, QUAD)
                if feed and not project:
                    pe.wait_ge(x2_lo_done, 2 * n)
                    if attend:
                        next(feed)

            def step_with_lo(n, u, it, **parts):
                step(n, u, it, with_lo=True, **parts)

            pe.wait_ge(lo_known, 1)
            has_lo = pe.value_load(lo_sum[0:1, 1:2].bitcast(I32))
            with pe.If(has_lo != 0):
                first_steps(step_with_lo)
                middle_steps(pe, step_with_lo, feed)
            with pe.Else():
                first_steps(step)
                middle_steps(pe, step, feed)
            last_steps(step, feed)

        return sync, gpsimd, vector, scalar, tensor, ff_raw, x1_out, x2_out


def feed_forward(nc, g):
    C, T, E, NB, FT, REST, SB, HALVES, GROUP, ST_BLOCK = (g[k] for k in "C T E NB FT REST SB HALVES GROUP ST_BLOCK".split())
    bank, ident, sem = g["bank"], g["ident"], g["sem"]
    absmax, compare_bias, power = (g[k] for k in "absmax compare_bias power".split())
    top, top_all, pow2, inv_pow2, w_scale, un_scale = (g[k] for k in "top top_all pow2 inv_pow2 w_scale un_scale".split())
    x1_dram, x2_hi_dram, x2_lo_dram, out = (g[k] for k in "x1_dram x2_hi_dram x2_lo_dram out".split())
    w1, w2, w3 = g["w1"], g["w2"], g["w3"]
    out_dram = out.rearrange("a s e -> (a s) e")
    GATE, UP, DOWN, TURN = 0, 2, 4, 6
    ROUNDS = (FT + 1) // GROUP

    UNIT = ((0, 0), (1, 0), (0, 1), (1, 1), (2, 0), (2, 1), (0, 2), (1, 2), (0, 3))
    AHEAD = 3
    WINDOWS = 6
    STEP_STARTS = (0, 17, 34, 50, 66, 78, 6 * LEVELS)

    with ExitStack() as mine:
        def sb(name, shape, dt=F32):
            return mine.enter_context(nc.sbuf_tensor(name, shape, dt))

        inv_absmax = sb("inv_absmax", [P, FT + 1, 3, NB])
        codes = sb("codes", [P, 2, E])
        w12T_hi = sb("w12T_hi", [P, 2, 2, C, P], F16)
        w12T_lo = sb("w12T_lo", [P, 2, 2, C, P], F16)
        w3T_hi = sb("w3T_hi", [P, 2, E], F16)
        w3T_lo = sb("w3T_lo", [P, 2, E], F16)
        hT_hi = sb("hT_hi", [P, 2, SB * BANK], F16)
        hidden = sb("hidden", [P, 2, BANK])
        w_nat = sb("w_nat", [P, 2, E])
        signs = sb("signs", [P, SIGN_RING, E], I8)
        hT_lo = sb("hT_lo", [P, 2, SB * BANK], F16)
        down_part = sb("down_part", [P, 2, BANK])
        x2T_hi = sb("x2T_hi", [P, T, C, P], F16)
        x2T_lo = sb("x2T_lo", [P, T, C, P], F16)
        acc = sb("acc", [P, T, E])

        spare = g["ff_raw"]
        squares = spare[:, 0:(FT + 1) * 2 * NB].rearrange("p (t m b) -> p t m b", m=2, b=NB)
        norms = spare[:, (FT + 1) * 2 * NB:][:, 0:(FT + 1) * 2].rearrange("p (t m) -> p t m", m=2)
        norm_prod = spare[:, (FT + 1) * 2 * (NB + 1):][:, 0:FT + 1]

        seq = Count(sem("scale_seq"))
        inv_ready = sem("inv_ready")
        ff_max = sem("ff_max")
        ff_max_all = sem("ff_max_all")
        ff_floor = sem("ff_floor")
        ff_root = sem("ff_root")
        scaled = sem("scaled")
        x2_in = [sem(f"x2_in{b}") for b in range(SB)]
        acc_in = sem("acc_in")
        w_in = [sem("ffw_in0"), sem("ffw_in1")]
        divided = sem("divided")
        held = sem("held3")
        sign_set = sem("sign_set")
        left_sum = sem("left_sum")
        sign_used = sem("sign_used")
        rounded = sem("rounded")
        w_turned = sem("ffw_turned")
        w_hi_done = sem("ffw_hi_done")
        w_lo_done = sem("ffw_lo_done")
        gate_done = sem("gate_done")
        up_done = sem("up_done")
        silu_done = sem("silu_done")
        hidden_done = [sem("hidden_done0"), sem("hidden_done1")]
        h_hi_done = sem("h_hi_done")
        h_lo_done = [sem("h_lo_done0"), sem("h_lo_done1")]
        down_read = [sem("down_read0"), sem("down_read1")]
        down_done = [sem("down_done0"), sem("down_done1")]
        summed = sem("summed")
        stored = sem("stored")

        def down_bank(st, h):
            return bank[:, (GATE, UP)[h]] if st % 2 == 0 else bank[:, DOWN + h]

        def rows_of(m, size):
            return (size, E) if m < 2 else (P, C * size)

        def per_block(table, r, v, size):
            m, ahead = UNIT[v]
            rows, cols = rows_of(m, size)
            if size == P:
                part = table[:].rearrange("p t m b -> p (t m b)")[:, bass.ds((r * 2 + ahead) * (3 * NB) + m * NB, NB)]
            else:
                part = table[0:rows, r * 2 + ahead, m, 0:NB] if m < 2 else table[:, r * 2 + ahead, m, 0::P // size]
            return part.unsqueeze(2).to_broadcast([rows, cols // BLOCK, BLOCK])

        def rounds(eng, body):
            with eng.Fori(0, ROUNDS - 2) as r:
                body(r, FULL)
            body(ROUNDS - 2, (P, P, P, REST))
            body(ROUNDS - 1, (P, REST, 0, 0))

        def size_of(v, sizes):
            return sizes[UNIT[v][1]] if v < len(UNIT) else 0

        def steps_of(w, sizes):
            steps = [divmod(at, LEVELS) for at in range(STEP_STARTS[w], STEP_STARTS[w + 1])]
            return [(AHEAD + v, k) for v, k in steps if size_of(AHEAD + v, sizes)]

        FULL = (P, P, P, P)
        first_units = [[(v, k) for k in range(LEVELS)] for v in range(AHEAD)]

        def portion(steps, i, n):
            return steps[i * len(steps) // n:(i + 1) * len(steps) // n]

        def ring(v, k):
            return (LEVELS * v + k) % SIGN_RING

        def split_parts(w12T, w3T, m, par, h, size):
            if m == 1 and size < P:
                return (w12T[:, par, 0, 4 * h:4 * h + 4, size:2 * size],
                        bank[:, TURN + h].rearrange("p (c s) -> p c s", s=P)[:, :, 0:size])
            if m < 2:
                return (w12T[:, par, m, 4 * h:4 * h + 4, 0:size],
                        bank[:, TURN + h].rearrange("p (c s) -> p c s", s=P)[:, :, 0:size])
            return w3T[0:size, par, h * BANK:(h + 1) * BANK], bank[0:size, TURN + h]

        def sync(sp):
            def load(r, v, size):
                m, ahead = UNIT[v]
                rows, cols = rows_of(m, size)
                unit, slot = r * 6 + v, v % 2
                first = (r * 2 + ahead) * P
                if v >= 2:
                    sp.wait_ge(sign_set, (unit - 1) * LEVELS)
                    if m == 2:
                        sp.sem_inc(held, 1)
                if m < 2:
                    sp.dma_start(w_nat[0:rows, slot], (w1, w2)[m][bass.ds(first, rows), :]).then_inc(w_in[slot], 16)
                else:
                    sp.dma_start(w_nat[:, slot, 0:cols].rearrange("p (t h) -> p t h", t=C),
                                 w3.rearrange("(t p) h -> p t h", p=P)[:, :, bass.ds(first, size)]).then_inc(w_in[slot], 16)

            def body(r, sizes):
                for w in range(WINDOWS):
                    v = AHEAD + 1 + w
                    if w + 1 < WINDOWS and size_of(v, sizes):
                        load(r, v, size_of(v, sizes))
                    elif w + 1 == WINDOWS and sizes[3]:
                        load(r + 1, AHEAD, sizes[3])

            def load_tokens(b):
                tiles = slice(b * ST_BLOCK, (b + 1) * ST_BLOCK)
                for part, dram in ((x2T_hi, x2_hi_dram), (x2T_lo, x2_lo_dram)):
                    sp.dma_start(part[:, tiles].rearrange("p t c s -> p t (c s)"),
                                 dram.rearrange("(t p) f -> p t f", p=P)[:, tiles]).then_inc(x2_in[b], 16)

            for v in range(2):
                load(0, v, P)
            yield
            load_tokens(0)
            yield
            load(0, 2, P)
            for b in range(1, SB - 1):
                load_tokens(b)
            yield
            load(0, 3, P)
            yield
            load_tokens(SB - 1)
            rounds(sp, body)
            for st in range(T):
                sp.wait_ge(down_read[0], (ROUNDS - 1) * T + st + 3)
                sp.wait_ge(summed, (ROUNDS - 1) * T + st + 1 + 2)
                sp.dma_start(out_dram[st * P:(st + 1) * P, :], acc[:, st]).then_inc(stored, 16)
            sp.wait_ge(stored, 16 * T)

        def gpsimd(pool):
            def divide(r, v, size):
                m, _ = UNIT[v]
                rows, cols = rows_of(m, size)
                slot = v % 2
                pool.wait_ge(w_in[slot], (r * 3 + v // 2 + 1) * 16)
                part = w_nat[0:rows, slot, 0:cols].rearrange("p (b e) -> p b e", e=BLOCK)
                nc.gpsimd.tensor_tensor(part, part, per_block(inv_absmax, r, v, size), ALU.mult).then_inc(divided, 1)

            def times_absmax(r, v, size):
                rows, cols = rows_of(UNIT[v][0], size)
                pool.wait_ge(sign_used, (r * 6 + v + 1) * LEVELS + SIGN_RING)
                part = codes[0:rows, v % 2, 0:cols].rearrange("p (b e) -> p b e", e=BLOCK)
                nc.gpsimd.tensor_tensor(part, part, per_block(absmax, r, v, size), ALU.mult).then_inc(rounded, 1)

            def hidden_lo(r, p, sb_, rows):
                tile, par = r * 2 + p, sb_ % 2
                cols = slice(sb_ * BANK, (sb_ + 1) * BANK)
                pool.wait_ge(h_hi_done, tile * SB + sb_ + 1)
                nc.gpsimd.tensor_tensor(hT_lo[0:rows, p, cols], hidden[0:rows, par], hT_hi[0:rows, p, cols],
                                        ALU.subtract).then_inc(h_lo_done[par], 1)

            def add_down(r, st):
                pool.wait_ge(acc_in, 16 * SB)
                pool.wait_ge(down_read[1], r * T + st + 3)
                nc.gpsimd.tensor_tensor(acc[:, st, BANK:], acc[:, st, BANK:], down_part[:, st % 2], ALU.add).then_inc(summed, 1)

            def body(r, sizes):
                for w in range(WINDOWS):
                    v = AHEAD + w
                    if w + 1 < WINDOWS and size_of(v + 1, sizes):
                        divide(r, v + 1, size_of(v + 1, sizes))
                    elif w + 1 == WINDOWS and sizes[3]:
                        divide(r + 1, AHEAD, sizes[3])
                    if w < 4:
                        hidden_lo(r, w // 2, w % 2 * 2, sizes[w // 2])
                        if size_of(v, sizes):
                            times_absmax(r, v, size_of(v, sizes))
                        hidden_lo(r, w // 2, w % 2 * 2 + 1, sizes[w // 2])
                    else:
                        for i in range(T // 2):
                            add_down(r, (w - 4) * (T // 2) + i)
                        if size_of(v, sizes):
                            times_absmax(r, v, size_of(v, sizes))

            pool.sem_inc(summed, 2)
            pool.wait_ge(ff_max, 1)
            nc.gpsimd.partition_all_reduce(top_all[:], top[:], P, ALL_MAX).then_inc(ff_max_all, 1)
            pool.wait_ge(inv_ready, 1)
            divide(0, 0, P)
            pool.wait_ge(ff_floor, 1)
            nc.gpsimd.tensor_tensor(top_all[:, 3:4], pow2[:, 3:4], power[:, 1:2], ALU.pow).then_inc(ff_root, 1)
            divide(0, 1, P)
            yield
            pool.wait_ge(scaled, 1)
            times_absmax(0, 0, P)
            yield
            for v in range(1, AHEAD):
                divide(0, v + 1, P)
                times_absmax(0, v, P)
            pool.wait_ge(inv_ready, 3)
            rounds(pool, body)

        def scalar(act):
            def compare(r, steps, sizes):
                for v, k in steps:
                    size = size_of(v, sizes)
                    rows, cols = rows_of(UNIT[v][0], size)
                    unit = r * 6 + v
                    if k == 0:
                        act.wait_ge(divided, unit + 1)
                    act.wait_ge(sign_used, unit * LEVELS + k + 1)
                    nc.scalar.activation(signs[0:rows, ring(v, k), 0:cols], w_nat[0:rows, v % 2, 0:cols], ACT.Sign,
                                         scale=COMPARE[k][0], bias=compare_bias[0:rows, k:k + 1]).then_inc(sign_set, 1)

            def turned_hi(r, v, size):
                m, ahead = UNIT[v]
                par = ahead % 2
                for h in range(HALVES):
                    act.wait_ge(w_turned, (r * 6 + v) * HALVES + h + 1)
                    dst, src = split_parts(w12T_hi, w3T_hi, m, par, h, size)
                    nc.scalar.activation(dst, src, ACT.Copy).then_inc(w_hi_done, 1)

            def silu(r, p, sb_, rows):
                tile, par = r * 2 + p, sb_ % 2
                act.wait_ge(gate_done, tile * SB + sb_ + 1)
                act.wait_ge(h_lo_done[par], tile * 2 + sb_ // 2 + 1)
                nc.scalar.activation(hidden[0:rows, par], bank[0:rows, GATE + par], ACT.Silu,
                                     scale=un_scale[0:rows, 0:1]).then_inc(silu_done, 1)

            def hidden_hi(r, p, sb_, rows):
                tile, par = r * 2 + p, sb_ % 2
                act.wait_ge(hidden_done[par], tile * 2 + sb_ // 2 + 2)
                nc.scalar.activation(hT_hi[0:rows, p, sb_ * BANK:(sb_ + 1) * BANK], hidden[0:rows, par], ACT.Copy).then_inc(h_hi_done, 1)

            def drain(r, st):
                act.wait_ge(down_done[1], r * T + st + 1)
                act.wait_ge(summed, r * T + st + 1)
                nc.scalar.activation(down_part[:, st % 2], down_bank(st, 1), ACT.Copy,
                                     scale=un_scale[:, 2:3]).then_inc(down_read[1], 1)

            def body(r, sizes):
                for w in range(WINDOWS):
                    v = AHEAD + w
                    steps, turn = steps_of(w, sizes), size_of(v - 1, sizes)
                    if w < 4:
                        compare(r, portion(steps, 0, 4), sizes)
                        if w > 0:
                            hidden_hi(r, (w - 1) // 2, (w - 1) % 2 * 2 + 1, sizes[(w - 1) // 2])
                        compare(r, portion(steps, 1, 4), sizes)
                        silu(r, w // 2, w % 2 * 2, sizes[w // 2])
                        if turn:
                            turned_hi(r, v - 1, turn)
                        compare(r, portion(steps, 2, 4), sizes)
                        hidden_hi(r, w // 2, w % 2 * 2, sizes[w // 2])
                        compare(r, portion(steps, 3, 4), sizes)
                        silu(r, w // 2, w % 2 * 2 + 1, sizes[w // 2])
                        continue
                    tiles = T // 2
                    for i in range(tiles):
                        compare(r, portion(steps, i, tiles), sizes)
                        if w == 4 and i == 1:
                            hidden_hi(r, 1, SB - 1, sizes[1])
                        drain(r, (w - 4) * tiles + i)
                        if i == tiles // 2 - 1 and turn:
                            turned_hi(r, v - 1, turn)

            compare(0, first_units[0][:2], FULL)
            yield
            compare(0, first_units[0][2:5], FULL)
            yield
            compare(0, first_units[0][5:7], FULL)
            yield
            compare(0, first_units[0][7:9], FULL)
            yield
            compare(0, first_units[0][9:], FULL)
            compare(0, first_units[1][:8], FULL)
            turned_hi(0, 0, P)
            compare(0, first_units[1][8:], FULL)
            yield
            turned_hi(0, 1, P)
            compare(0, first_units[2][:6], FULL)
            act.wait_ge(g["x1_out"], 16 * T)
            act.wait_ge(g["x2_out"], 32 * (T + 1))
            for b in range(SB):
                tiles = slice(b * ST_BLOCK, (b + 1) * ST_BLOCK)
                act.dma_start(acc[:, tiles], x1_dram.rearrange("(t p) e -> p t e", p=P)[:, tiles]).then_inc(acc_in, 16)
            compare(0, first_units[2][6:], FULL)
            rounds(act, body)

        def vector(dve):
            V = nc.vector

            def sum_steps(r, steps, sizes):
                for v, k in steps:
                    rows, cols = rows_of(UNIT[v][0], size_of(v, sizes))
                    unit = r * 6 + v
                    total = codes[0:rows, v % 2, 0:cols]
                    dve.wait_ge(sign_set, unit * LEVELS + k + 1)
                    part = signs[0:rows, ring(v, k), 0:cols]
                    if k == 0 and v >= 2:
                        dve.wait_ge(w_turned, (unit - 1) * HALVES)
                    for h, (done, credit) in enumerate(((left_sum, 0), (sign_used, SIGN_RING))):
                        half = slice(h * cols // 2, (h + 1) * cols // 2)
                        if k == 0:
                            V.tensor_scalar(total[:, half], part[:, half], HALF_STEP[0], None, ALU.mult).then_inc(done, 1)
                        else:
                            dve.wait_ge(done, unit * LEVELS + credit + k)
                            V.scalar_tensor_tensor(total[:, half], part[:, half], HALF_STEP[k], total[:, half],
                                                   ALU.mult, ALU.add).then_inc(done, 1)

            def turned_lo(r, v, size):
                m, ahead = UNIT[v]
                par = ahead % 2
                for h in range(HALVES):
                    dve.wait_ge(w_hi_done, (r * 6 + v) * HALVES + h + 1)
                    hi, src = split_parts(w12T_hi, w3T_hi, m, par, h, size)
                    lo, _ = split_parts(w12T_lo, w3T_lo, m, par, h, size)
                    V.tensor_tensor(lo, src, hi, ALU.subtract).then_inc(w_lo_done, 1)

            def hidden_value(r, p, sb_, rows):
                tile, par = r * 2 + p, sb_ % 2
                dve.wait_ge(silu_done, tile * SB + sb_ + 1)
                if rows == P:
                    dve.wait_ge(up_done, tile * SB + sb_ + 1)
                up = bank[0:rows, UP + par] if rows == P else bank[rows:2 * rows, GATE + par]
                V.scalar_tensor_tensor(hidden[0:rows, par], up, un_scale[0:rows, 1:2], hidden[0:rows, par],
                                       ALU.mult, ALU.mult).then_inc(hidden_done[par], 1)

            def then(ins):
                seq.mark(ins)
                seq.wait(dve)

            def look_at_scales():
                for m in range(3):
                    then(V.tensor_reduce(top[:, m:m + 1], absmax[:, :, m], AX.XY, ALU.max))
                then(V.tensor_tensor(squares, absmax[:, :, 0:2], absmax[:, :, 0:2], ALU.mult))
                then(V.tensor_reduce(norms, squares, AX.X, ALU.add))
                then(V.tensor_tensor(norm_prod, norms[:, :, 0], norms[:, :, 1], ALU.mult))
                V.tensor_reduce(top[:, 3:4], norm_prod, AX.X, ALU.max).then_inc(ff_max, 1)

            def invert(first, last):
                tiles = slice(first, last)
                V.reciprocal(inv_absmax[:, tiles], inv_absmax[:, tiles]).then_inc(inv_ready, 1)

            def first_reciprocals():
                then(V.tensor_scalar(inv_absmax[:], absmax[:], TINY, None, ALU.max))
                invert(0, 2)

            def floor_scales():
                dve.wait_ge(ff_max_all, 1)
                V.tensor_scalar(pow2[:], top_all[:], TINY, None, ALU.max).then_inc(ff_floor, 1)

            def set_scales():
                dve.wait_ge(ff_root, 1)
                then(V.tensor_copy(pow2[:, 3:4], top_all[:, 3:4]))
                then(V.tensor_scalar(pow2[:].bitcast(I32), pow2[:].bitcast(I32), EXPONENT_BITS, None, ALU.bitwise_and))
                then(V.reciprocal(inv_pow2[:], pow2[:]))
                then(V.tensor_scalar(w_scale[:, 0:3], inv_pow2[:, 0:3], 2.0 ** 14, None, ALU.mult))
                for m in range(3):
                    last = V.tensor_scalar(absmax[:, :, m], absmax[:, :, m], w_scale[:, m:m + 1], None, ALU.mult)
                last.then_inc(scaled, 1)

            def set_un_scales():
                then(V.tensor_scalar(un_scale[:, 0:2], pow2[:, 0:2], 2.0 ** -14 / X_SCALE, None, ALU.mult))
                then(V.tensor_scalar(un_scale[:, 1:2], un_scale[:, 1:2], inv_pow2[:, 3:4], 2.0 ** -2, ALU.mult, ALU.mult))
                then(V.tensor_scalar(un_scale[:, 2:3], pow2[:, 2:3], pow2[:, 3:4], 2.0 ** (2 - 14), ALU.mult, ALU.mult))

            def add_down(r, st):
                dve.wait_ge(acc_in, 16 * SB)
                dve.wait_ge(down_done[0], r * T + st + 1)
                V.scalar_tensor_tensor(acc[:, st, 0:BANK], down_bank(st, 0), un_scale[:, 2:3], acc[:, st, 0:BANK],
                                       ALU.mult, ALU.add).then_inc(down_read[0], 1)

            def body(r, sizes):
                for w in range(WINDOWS):
                    v = AHEAD + w
                    steps, turn = steps_of(w, sizes), size_of(v - 1, sizes)
                    if w < 4:
                        sum_steps(r, portion(steps, 0, 2), sizes)
                        hidden_value(r, w // 2, w % 2 * 2, sizes[w // 2])
                        if turn:
                            turned_lo(r, v - 1, turn)
                        sum_steps(r, portion(steps, 1, 2), sizes)
                        hidden_value(r, w // 2, w % 2 * 2 + 1, sizes[w // 2])
                        continue
                    tiles = T // 2
                    for i in range(tiles):
                        add_down(r, (w - 4) * tiles + i)
                        sum_steps(r, portion(steps, i, tiles), sizes)
                        if i == tiles // 2 - 1 and turn:
                            turned_lo(r, v - 1, turn)

            look_at_scales()
            for i in range(2):
                dve.sem_inc(hidden_done[i], 1)
                dve.sem_inc(h_lo_done[i], 1)
                dve.sem_inc(down_read[i], 2)
            dve.sem_inc(sign_used, SIGN_RING)
            yield
            first_reciprocals()
            yield
            floor_scales()
            yield
            set_scales()
            sum_steps(0, first_units[0][:3], FULL)
            yield
            set_un_scales()
            sum_steps(0, first_units[0][3:6], FULL)
            invert(2, FT // 2)
            yield
            sum_steps(0, first_units[0][6:8], FULL)
            yield
            yield
            invert(FT // 2, FT + 1)
            sum_steps(0, first_units[0][8:], FULL)
            yield
            sum_steps(0, first_units[1][:8], FULL)
            yield
            turned_lo(0, 0, P)
            sum_steps(0, first_units[1][8:12], FULL)
            yield
            sum_steps(0, first_units[1][12:], FULL)
            yield
            turned_lo(0, 1, P)
            sum_steps(0, first_units[2], FULL)
            rounds(dve, body)

        def tensor(pe):
            def turn(r, v, size):
                m, _ = UNIT[v]
                unit, slot = r * 6 + v, v % 2
                pe.wait_ge(rounded, unit + 1)
                pe.wait_ge(w_lo_done, unit * HALVES)
                for h in range(HALVES):
                    for c in range(4 * h, 4 * h + 4):
                        if m < 2:
                            last = nc.tensor.transpose(bank[:, TURN + h, c % 4 * P:c % 4 * P + size],
                                                       codes[0:size, slot, c * P:(c + 1) * P], ident[0:size, 0:size])
                        else:
                            last = nc.tensor.transpose(bank[0:size, TURN + h, c % 4 * P:(c % 4 + 1) * P],
                                                       codes[:, slot, c * size:(c + 1) * size], ident[:])
                    last.then_inc(w_turned, 1)

            def gate_up(r, p, sb_, rows):
                tile, par = r * 2 + p, sb_ % 2
                toks = slice(sb_ * ST_BLOCK, (sb_ + 1) * ST_BLOCK)
                pe.wait_ge(x2_in[sb_], 32)
                pe.wait_ge(hidden_done[par], tile * 2 + sb_ // 2 + 1)
                if p == 0 and sb_ == 0:
                    for h in range(HALVES):
                        pe.wait_ge(down_read[h], r * T + 1)
                if rows < P:
                    products = ((0, GATE, gate_done, 2 * rows),)
                else:
                    products = ((0, GATE, gate_done, P), (1, UP, up_done, P))
                for m, to, done, outs in products:
                    if sb_ == 0:
                        units = 2 * p + m + 1 if rows == P else 2 * p + 2
                        pe.wait_ge(w_lo_done, (r * 6 + units) * HALVES)
                    dst = bank[0:outs, to + par]
                    for c in range(C):
                        hi, lo = w12T_hi[:, p, m, c, 0:outs], w12T_lo[:, p, m, c, 0:outs]
                        nc.tensor.matmul(dst, hi, x2T_hi[:, toks, c], start=c == 0, stop=False)
                        nc.tensor.matmul(dst, hi, x2T_lo[:, toks, c], start=False, stop=False)
                        last = nc.tensor.matmul(dst, lo, x2T_hi[:, toks, c], start=False, stop=c == C - 1)
                    last.then_inc(done, 1)

            def down(r, st, rows):
                toks = slice(st * P, (st + 1) * P)
                if st % ST_BLOCK == 0:
                    sb_ = st // ST_BLOCK
                    pe.wait_ge(h_lo_done[sb_ % 2], (r * 2 + 1) * 2 + sb_ // 2 + 2)
                if st == 0:
                    pe.wait_ge(hidden_done[0], (r * 2 + 1) * 2 + 3)
                for h in range(HALVES):
                    cols = slice(h * BANK, (h + 1) * BANK)
                    pe.wait_ge(down_read[h], r * T + st + 1)
                    for p in range(GROUP):
                        k = slice(0, rows[p])
                        dst = down_bank(st, h)
                        nc.tensor.matmul(dst, hT_hi[k, p, toks], w3T_hi[k, p, cols], start=p == 0, stop=False)
                        nc.tensor.matmul(dst, hT_hi[k, p, toks], w3T_lo[k, p, cols], start=False, stop=False)
                        last = nc.tensor.matmul(dst, hT_lo[k, p, toks], w3T_hi[k, p, cols], start=False, stop=p == GROUP - 1)
                    last.then_inc(down_done[h], 1)

            def body(r, sizes):
                for w in range(WINDOWS):
                    v = AHEAD - 1 + w
                    size = size_of(v, sizes)
                    if w < 4:
                        gate_up(r, w // 2, w % 2 * 2, sizes[w // 2])
                        if size:
                            turn(r, v, size)
                        gate_up(r, w // 2, w % 2 * 2 + 1, sizes[w // 2])
                        continue
                    if w == 4:
                        pe.wait_ge(w_lo_done, (r * 6 + 6) * HALVES)
                    for i in range(T // 2):
                        down(r, (w - 4) * (T // 2) + i, sizes[0:GROUP])
                        if i == T // 4 - 1 and size:
                            turn(r, v, size)

            turn(0, 0, P)
            pe.wait_ge(w_lo_done, HALVES)
            yield
            turn(0, 1, P)
            rounds(pe, body)

        return sync, gpsimd, vector, scalar, tensor


_INS = ["L0_attn_hidden_states", "L0_attn_wq", "L0_attn_bq", "L0_attn_wk", "L0_attn_bk", "L0_attn_wv", "L0_attn_bv",
        "L0_ffn_w1", "L0_ffn_w2", "L0_ffn_w3"]


def kernel(**inputs):
    import concourse.bacc as bacc
    from concourse.bass_utils import run_bass_kernel_spmd

    nc = bacc.Bacc("TRN2", target_bir_lowering=False, num_devices=1)
    arrays, args = {}, []
    for name in _INS:
        a = np.ascontiguousarray(inputs[name])
        arrays[f"in_{name}"] = a
        args.append(nc.dram_tensor(f"in_{name}", a.shape, mybir.dt.from_np(a.dtype), kind="ExternalInput").ap())
    shape = arrays["in_L0_attn_hidden_states"].shape
    out = nc.dram_tensor("out", shape, F32, kind="ExternalOutput").ap()
    layer(nc, *args, out)
    r = run_bass_kernel_spmd(nc, [arrays], core_ids=[0])
    return r.results[0]["out"]
```
